# Optimizing a Trainium2 kernel written in Bass

```python
import numpy as np
import jax
import jax.numpy as jnp

def _softmax(x, axis=-1):
    return jax.nn.softmax(x, axis=axis)

def _gelu(x):
    return jax.nn.gelu(x, approximate=True)

def _silu(x):
    return jax.nn.silu(x)

def _sigmoid(x):
    return jax.nn.sigmoid(x)

def _layernorm(x, axis=-1, eps=1e-05):
    m = jnp.mean(x, axis=axis, keepdims=True)
    v = jnp.var(x, axis=axis, keepdims=True)
    return (x - m) / jnp.sqrt(v + eps)

def _scatter_add(tgt, idx, src, axis=0):
    return tgt.at[idx].add(src)

def _segment_sum(src, seg, n):
    return jax.ops.segment_sum(src, seg, n)
kernel_name = 'mk_seq_preln_d1_jaxref_r8_848b58'

def setup_inputs(seed: int=0):
    np.random.seed(seed)
    _w = jnp.asarray

    def _L0_attn_setup():
        import jax, jax.numpy as jnp
        import numpy as np
        EMBED_DIM = 128
        NUM_HEADS = 16
        HEAD_DIM = EMBED_DIM // NUM_HEADS

        def _sinusoid_pos_emb(seq_len, dim):
            pos = jnp.arange(seq_len, dtype=jnp.float32)
            idx = jnp.arange(dim // 2, dtype=jnp.float32)
            inv_freq = 1.0 / 10000.0 ** (2.0 * idx / dim)
            ang = pos[:, None] * inv_freq[None, :]
            return jnp.concatenate([jnp.sin(ang), jnp.cos(ang)], axis=-1)

        def _relative_shift(x):
            b, h, s, _ = x.shape
            x = jnp.pad(x, ((0, 0), (0, 0), (0, 0), (1, 0)))
            x = x.reshape(b, h, s + 1, s)
            return x[:, :, 1:, :].reshape(b, h, s, s)
        key = jax.random.key(seed)
        ks = jax.random.split(key, 12)
        D = EMBED_DIM
        sc = 1.0 / np.sqrt(D)
        inp = {'x': jax.random.normal(ks[0], (2, 256, D), dtype=jnp.float32)}
        for i, name in enumerate(['Wq', 'Wk', 'Wv', 'Wp', 'Wo']):
            inp[name] = jax.random.normal(ks[1 + i], (D, D), dtype=jnp.float32) * sc
            inp['b' + name[1].lower()] = jnp.zeros((D,), dtype=jnp.float32)
        inp['u'] = jax.random.normal(ks[6], (1, NUM_HEADS, 1, HEAD_DIM), dtype=jnp.float32) * 0.05
        inp['v'] = jax.random.normal(ks[7], (1, NUM_HEADS, 1, HEAD_DIM), dtype=jnp.float32) * 0.05
        return inp
    _L0_attn_in = _L0_attn_setup()

    def _L0_ffn_setup():
        import jax, jax.numpy as jnp
        import numpy as np
        DIM = 128
        DEPTH = 6
        HEADS = 16
        DIM_HEAD = 64
        WINDOW = 32
        INNER = HEADS * DIM_HEAD
        DIM_INNER = int(DIM * 4 * 2 / 3)
        QK_SCALE = 8.0

        def shift_tokens(t):
            a, s = jnp.split(t, 2, -1)
            s = jnp.pad(s, ((0, 0), (1, 0), (0, 0)))[:, :-1]
            return jnp.concatenate([a, s], -1)

        def l2norm(t):
            return t / jnp.maximum(jnp.linalg.norm(t, axis=-1, keepdims=True), 1e-12)

        def rotate_half(x):
            x1, x2 = jnp.split(x, 2, -1)
            return jnp.concatenate([-x2, x1], -1)

        def rotary_tables(n):
            half = jnp.arange(0, DIM_HEAD, 2, dtype=jnp.float32)
            inv_freq = 1.0 / 10000.0 ** (half / DIM_HEAD)
            t = jnp.arange(n, dtype=jnp.float32)
            freqs = t[:, None] * inv_freq[None, :]
            freqs = jnp.concatenate([freqs, freqs], -1)
            base_scale = (half + 0.4 * DIM_HEAD) / (1.4 * DIM_HEAD)
            power = (t - n // 2) / (WINDOW // 2)
            scale = base_scale[None, :] ** power[:, None]
            scale = jnp.concatenate([scale, scale], -1)
            return (freqs, scale)

        def local_attention(q, k, v):
            b, h, n, d = q.shape
            w = WINDOW
            nw = n // w
            bq = q.reshape(b, h, nw, w, d)
            bk = k.reshape(b, h, nw, w, d)
            bv = v.reshape(b, h, nw, w, d)

            def look(t):
                p = jnp.pad(t, ((0, 0), (0, 0), (1, 0), (0, 0), (0, 0)))
                return jnp.concatenate([p[:, :, :nw], p[:, :, 1:]], axis=3)
            bk2, bv2 = (look(bk), look(bv))
            seq = jnp.arange(n).reshape(nw, w)
            seq_p = jnp.pad(seq, ((1, 0), (0, 0)), constant_values=-1)
            jt = jnp.concatenate([seq_p[:nw], seq_p[1:]], axis=1)
            it = seq[:, :, None]
            jb = jt[:, None, :]
            mask = (it < jb) | (it > jb + w) | (jb == -1)
            sim = jnp.einsum('bhwie,bhwje->bhwij', bq, bk2) * QK_SCALE
            sim = jnp.where(mask, -jnp.finfo(sim.dtype).max, sim)
            attn = jax.nn.softmax(sim, -1)
            out = jnp.einsum('bhwij,bhwje->bhwie', attn, bv2)
            return out.reshape(b, h, n, d)

        def attn_layer(x, Wqkv, qs, ksc, Wo):
            b, n, _ = x.shape
            qkv = x @ Wqkv
            q, k, v = jnp.split(qkv, 3, -1)
            sh = lambda t: t.reshape(b, n, HEADS, DIM_HEAD).transpose(0, 2, 1, 3)
            q, k, v = (sh(q), sh(k), sh(v))
            q = l2norm(q) * qs
            k = l2norm(k) * ksc
            freqs, scale = rotary_tables(n)
            cos, sin = (jnp.cos(freqs), jnp.sin(freqs))
            q = q * cos * scale + rotate_half(q) * sin * scale
            inv = 1.0 / scale
            k = k * cos * inv + rotate_half(k) * sin * inv
            out = local_attention(q, k, v)
            out = out.transpose(0, 2, 1, 3).reshape(b, n, INNER)
            return out @ Wo

        def ffn_layer(x, g, bln, W1, b1, W2, b2):
            mu = x.mean(-1, keepdims=True)
            var = ((x - mu) ** 2).mean(-1, keepdims=True)
            xn = (x - mu) / jnp.sqrt(var + 1e-05) * g + bln
            hg = xn @ W1 + b1
            a, gate = jnp.split(hg, 2, -1)
            return a * jax.nn.gelu(gate, approximate=False) @ W2 + b2
        key = jax.random.key(seed)
        ks = jax.random.split(key, 8)
        B, N = (2, 256)
        init = lambda k, shape: jax.random.normal(k, shape, jnp.float32) * 0.02
        return {'x': jax.random.normal(ks[0], (B, N, DIM), jnp.float32), 'Wqkv': init(ks[1], (DEPTH, DIM, 3 * INNER)), 'q_scale': jnp.ones((DEPTH, DIM_HEAD), jnp.float32), 'k_scale': jnp.ones((DEPTH, DIM_HEAD), jnp.float32), 'Wo': init(ks[2], (DEPTH, INNER, DIM)), 'ln_g': jnp.ones((DEPTH, DIM), jnp.float32), 'ln_b': jnp.zeros((DEPTH, DIM), jnp.float32), 'W1': init(ks[3], (DEPTH, DIM, 2 * DIM_INNER)), 'b1': jnp.zeros((DEPTH, 2 * DIM_INNER), jnp.float32), 'W2': init(ks[4], (DEPTH, DIM_INNER, DIM)), 'b2': jnp.zeros((DEPTH, DIM), jnp.float32)}
    _L0_ffn_in = _L0_ffn_setup()
    _d = {'L0_attn_x': _L0_attn_in['x'], 'L0_attn_Wq': _L0_attn_in['Wq'], 'L0_attn_bq': _L0_attn_in['bq'], 'L0_attn_Wk': _L0_attn_in['Wk'], 'L0_attn_bk': _L0_attn_in['bk'], 'L0_attn_Wv': _L0_attn_in['Wv'], 'L0_attn_bv': _L0_attn_in['bv'], 'L0_attn_Wp': _L0_attn_in['Wp'], 'L0_attn_bp': _L0_attn_in['bp'], 'L0_attn_Wo': _L0_attn_in['Wo'], 'L0_attn_bo': _L0_attn_in['bo'], 'L0_attn_u': _L0_attn_in['u'], 'L0_attn_v': _L0_attn_in['v'], 'L0_ffn_Wqkv': _L0_ffn_in['Wqkv'], 'L0_ffn_q_scale': _L0_ffn_in['q_scale'], 'L0_ffn_k_scale': _L0_ffn_in['k_scale'], 'L0_ffn_Wo': _L0_ffn_in['Wo'], 'L0_ffn_ln_g': _L0_ffn_in['ln_g'], 'L0_ffn_ln_b': _L0_ffn_in['ln_b'], 'L0_ffn_W1': _L0_ffn_in['W1'], 'L0_ffn_b1': _L0_ffn_in['b1'], 'L0_ffn_W2': _L0_ffn_in['W2'], 'L0_ffn_b2': _L0_ffn_in['b2']}
    _x0 = _d['L0_attn_x']
    _d['L0_attn_x'] = jax.random.normal(jax.random.fold_in(jax.random.key(seed), 1), (4, 512, 128), dtype=_x0.dtype)
    del _x0
    return _d

def reference(L0_attn_x, L0_attn_Wq, L0_attn_bq, L0_attn_Wk, L0_attn_bk, L0_attn_Wv, L0_attn_bv, L0_attn_Wp, L0_attn_bp, L0_attn_Wo, L0_attn_bo, L0_attn_u, L0_attn_v, L0_ffn_Wqkv, L0_ffn_q_scale, L0_ffn_k_scale, L0_ffn_Wo, L0_ffn_ln_g, L0_ffn_ln_b, L0_ffn_W1, L0_ffn_b1, L0_ffn_W2, L0_ffn_b2):

    def _L0_attn_ref(x, Wq, bq, Wk, bk, Wv, bv, Wp, bp, Wo, bo, u, v):
        import jax, jax.numpy as jnp
        import numpy as np
        EMBED_DIM = 128
        NUM_HEADS = 16
        HEAD_DIM = EMBED_DIM // NUM_HEADS

        def _sinusoid_pos_emb(seq_len, dim):
            pos = jnp.arange(seq_len, dtype=jnp.float32)
            idx = jnp.arange(dim // 2, dtype=jnp.float32)
            inv_freq = 1.0 / 10000.0 ** (2.0 * idx / dim)
            ang = pos[:, None] * inv_freq[None, :]
            return jnp.concatenate([jnp.sin(ang), jnp.cos(ang)], axis=-1)

        def _relative_shift(x):
            b, h, s, _ = x.shape
            x = jnp.pad(x, ((0, 0), (0, 0), (0, 0), (1, 0)))
            x = x.reshape(b, h, s + 1, s)
            return x[:, :, 1:, :].reshape(b, h, s, s)
        B, S, D = x.shape
        H, P = (NUM_HEADS, HEAD_DIM)

        def heads(t):
            return t.reshape(B, S, H, P).transpose(0, 2, 1, 3)
        q = heads(x @ Wq + bq)
        k = heads(x @ Wk + bk)
        val = heads(x @ Wv + bv)
        pos = _sinusoid_pos_emb(S, D) @ Wp + bp
        pos = pos.reshape(S, H, P).transpose(1, 0, 2)
        content_score = jnp.einsum('bhsp,bhtp->bhst', q + u, k)
        pos_score = jnp.einsum('bhsp,htp->bhst', q + v, pos)
        pos_score = _relative_shift(pos_score)
        score = (content_score + pos_score) / jnp.sqrt(jnp.float32(P))
        weights = jax.nn.softmax(score, axis=-1)
        out = jnp.einsum('bhst,bhtp->bhsp', weights, val)
        out = out.transpose(0, 2, 1, 3).reshape(B, S, D)
        return out @ Wo + bo

    def _L0_ffn_ref(x, Wqkv, q_scale, k_scale, Wo, ln_g, ln_b, W1, b1, W2, b2):
        import jax, jax.numpy as jnp
        import numpy as np
        DIM = 128
        DEPTH = 6
        HEADS = 16
        DIM_HEAD = 64
        WINDOW = 32
        INNER = HEADS * DIM_HEAD
        DIM_INNER = int(DIM * 4 * 2 / 3)
        QK_SCALE = 8.0

        def shift_tokens(t):
            a, s = jnp.split(t, 2, -1)
            s = jnp.pad(s, ((0, 0), (1, 0), (0, 0)))[:, :-1]
            return jnp.concatenate([a, s], -1)

        def l2norm(t):
            return t / jnp.maximum(jnp.linalg.norm(t, axis=-1, keepdims=True), 1e-12)

        def rotate_half(x):
            x1, x2 = jnp.split(x, 2, -1)
            return jnp.concatenate([-x2, x1], -1)

        def rotary_tables(n):
            half = jnp.arange(0, DIM_HEAD, 2, dtype=jnp.float32)
            inv_freq = 1.0 / 10000.0 ** (half / DIM_HEAD)
            t = jnp.arange(n, dtype=jnp.float32)
            freqs = t[:, None] * inv_freq[None, :]
            freqs = jnp.concatenate([freqs, freqs], -1)
            base_scale = (half + 0.4 * DIM_HEAD) / (1.4 * DIM_HEAD)
            power = (t - n // 2) / (WINDOW // 2)
            scale = base_scale[None, :] ** power[:, None]
            scale = jnp.concatenate([scale, scale], -1)
            return (freqs, scale)

        def local_attention(q, k, v):
            b, h, n, d = q.shape
            w = WINDOW
            nw = n // w
            bq = q.reshape(b, h, nw, w, d)
            bk = k.reshape(b, h, nw, w, d)
            bv = v.reshape(b, h, nw, w, d)

            def look(t):
                p = jnp.pad(t, ((0, 0), (0, 0), (1, 0), (0, 0), (0, 0)))
                return jnp.concatenate([p[:, :, :nw], p[:, :, 1:]], axis=3)
            bk2, bv2 = (look(bk), look(bv))
            seq = jnp.arange(n).reshape(nw, w)
            seq_p = jnp.pad(seq, ((1, 0), (0, 0)), constant_values=-1)
            jt = jnp.concatenate([seq_p[:nw], seq_p[1:]], axis=1)
            it = seq[:, :, None]
            jb = jt[:, None, :]
            mask = (it < jb) | (it > jb + w) | (jb == -1)
            sim = jnp.einsum('bhwie,bhwje->bhwij', bq, bk2) * QK_SCALE
            sim = jnp.where(mask, -jnp.finfo(sim.dtype).max, sim)
            attn = jax.nn.softmax(sim, -1)
            out = jnp.einsum('bhwij,bhwje->bhwie', attn, bv2)
            return out.reshape(b, h, n, d)

        def attn_layer(x, Wqkv, qs, ksc, Wo):
            b, n, _ = x.shape
            qkv = x @ Wqkv
            q, k, v = jnp.split(qkv, 3, -1)
            sh = lambda t: t.reshape(b, n, HEADS, DIM_HEAD).transpose(0, 2, 1, 3)
            q, k, v = (sh(q), sh(k), sh(v))
            q = l2norm(q) * qs
            k = l2norm(k) * ksc
            freqs, scale = rotary_tables(n)
            cos, sin = (jnp.cos(freqs), jnp.sin(freqs))
            q = q * cos * scale + rotate_half(q) * sin * scale
            inv = 1.0 / scale
            k = k * cos * inv + rotate_half(k) * sin * inv
            out = local_attention(q, k, v)
            out = out.transpose(0, 2, 1, 3).reshape(b, n, INNER)
            return out @ Wo

        def ffn_layer(x, g, bln, W1, b1, W2, b2):
            mu = x.mean(-1, keepdims=True)
            var = ((x - mu) ** 2).mean(-1, keepdims=True)
            xn = (x - mu) / jnp.sqrt(var + 1e-05) * g + bln
            hg = xn @ W1 + b1
            a, gate = jnp.split(hg, 2, -1)
            return a * jax.nn.gelu(gate, approximate=False) @ W2 + b2
        for i in range(DEPTH):
            x = attn_layer(shift_tokens(x), Wqkv[i], q_scale[i], k_scale[i], Wo[i]) + x
            x = ffn_layer(shift_tokens(x), ln_g[i], ln_b[i], W1[i], b1[i], W2[i], b2[i]) + x
        return x
    x = L0_attn_x
    x = x + _L0_attn_ref(_layernorm(x, axis=-1), L0_attn_Wq, L0_attn_bq, L0_attn_Wk, L0_attn_bk, L0_attn_Wv, L0_attn_bv, L0_attn_Wp, L0_attn_bp, L0_attn_Wo, L0_attn_bo, L0_attn_u, L0_attn_v)
    x = x + _L0_ffn_ref(_layernorm(x, axis=-1), L0_ffn_Wqkv, L0_ffn_q_scale, L0_ffn_k_scale, L0_ffn_Wo, L0_ffn_ln_g, L0_ffn_ln_b, L0_ffn_W1, L0_ffn_b1, L0_ffn_W2, L0_ffn_b2)
    return x

_drawn_inputs = setup_inputs


def setup_inputs(seed=0):
    import zlib

    import numpy as np

    out = dict(_drawn_inputs(seed))
    spreads = {'L0_attn_bq': (0.0, 0.681),
     'L0_attn_bk': (0.0, 0.8),
     'L0_attn_bv': (0.0, 0.1),
     'L0_attn_bp': (0.0, 0.8),
     'L0_attn_bo': (0.0, 0.1),
     'L0_ffn_q_scale': (1.0, 0.6),
     'L0_ffn_k_scale': (1.0, 0.6),
     'L0_ffn_ln_g': (1.0, 0.6),
     'L0_ffn_ln_b': (0.0, 0.8),
     'L0_ffn_b1': (0.0, 0.8),
     'L0_ffn_b2': (0.0, 0.1)}
    factors = {'L0_attn_u': 8.0, 'L0_attn_v': 8.0, 'L0_ffn_W1': 3.638, 'L0_ffn_W2': 3.591}
    for name, (base, spread) in spreads.items():
        noise = np.random.default_rng([zlib.crc32(name.encode()), seed]).standard_normal(out[name].shape)
        drawn = base * np.exp(spread * noise) if base else spread * noise
        out[name] = jnp.asarray(drawn.astype(out[name].dtype))
    for name, factor in factors.items():
        out[name] = (out[name] * factor).astype(out[name].dtype)
    return out
```

```python
from contextlib import ExitStack

import concourse.bass as bass
from concourse import mybir

F32, BF16 = mybir.dt.float32, mybir.dt.bfloat16
ALU, ACT, AX = mybir.AluOpType, mybir.ActivationFunctionType, mybir.AxisListType

P = 128
D = 128
BATCH, SEQ = 4, 512
SEQT = SEQ // P
TILES = BATCH * SEQT
EPS = 1e-5

H0, DP = 16, 8
SCALE0 = DP ** -0.5

DEPTH, HEADS, DH, W = 6, 16, 64, 32
INNER = HEADS * DH
PAIRS = HEADS // 2
W2 = 2 * W
WT = P // W
DFF = int(D * 4 * 2 / 3)
FCH = 3
FW = -(-DFF // FCH)
QK_SCALE = 8.0
NORM_FLOOR = 1e-24
MASKED = -1e30


class Tally:

    def __init__(self, sem):
        self.sem, self.base, self.n = sem, 0, 0

    def add(self, ins):
        ins.then_inc(self.sem, 1)
        self.n += 1

    def settle(self, eng):
        eng.wait_ge(self.sem, self.base + self.n)

    def close(self):
        self.base, self.n = self.base + self.n, 0


def at_least(eng, sem, count):
    if not isinstance(count, int) or count > 0:
        eng.wait_ge(sem, count)


def stand(eng, sem):
    eng.sem_inc(sem, 1)


def rounds(eng, first, last, body, own=None, each=0):
    body(first)
    if own is not None:
        own.close()
        after_first = own.base
    with eng.Fori(first + 1, last) as g:
        if own is not None:
            own.base = eng.snap(after_first + (g - first - 1) * each)
        body(g)
    if own is not None:
        assert own.n == each, (own.n, each)
        own.base, own.n = after_first + (last - first - 1) * each, 0
    body(last)


def local_layers(nc, x, w):
    with ExitStack() as ctx:
        def sb(name, shape, dt=F32):
            return ctx.enter_context(nc.sbuf_tensor(name, shape, dt))

        wqkv = sb("wqkv", [P, 2, 3 * INNER])
        wo = sb("wo", [P, 2, PAIRS, D])
        w1ring = sb("w1ring", [P, 2, 2 * FCH * FW])
        w2 = sb("w2", [FW, 2, FCH, D])
        b1 = sb("b1", [FW, 2, 2 * FCH])
        ln = sb("ln", [P, 2, 2])
        b2 = sb("b2", [P, 2, D])
        qkscale = sb("qkscale", [P, 2, 2, DH])
        w1 = sb("w1", [P, 2 * FCH * FW])
        rope = sb("rope", [P, 2, SEQT * 2, DH])
        ropes = sb("ropes", [P, 2, 2, SEQT * 2, DH])
        ident = sb("ident_l", [P, P])
        identb = sb("identb", [P, P], BF16)
        bias = sb("bias", [P, 2, 8, W2], BF16)

        xs = sb("xs", [P, SEQT, D])
        xsf = sb("xsf", [P, SEQT, D])
        xT = sb("xT", [P, 2, P])
        squares = sb("squares", [P, INNER])
        turned = sb("turned", [P, 2, 2, INNER])
        roped = sb("roped", [P, 2, INNER])
        ss = sb("ss", [P, 2 * HEADS])
        rnorm = sb("rnorm", [P, 2, HEADS])
        power = sb("power", [P, HEADS])
        eps = sb("eps", [P, SEQT])
        qT = sb("qT", [P, PAIRS, P])
        kT = sb("kT", [P, 2, PAIRS, W + P])
        v = sb("v", [P, 2, INNER])
        vwin = sb("vwin", [P, 2 * WT, INNER // 2])
        probs = sb("probs", [P, 2, HEADS, W2])
        smax = sb("smax", [P, HEADS])
        rsum = sb("rsum", [P, 2, HEADS])
        pT = sb("pT", [P, PAIRS, P])
        oT = sb("oT", [P, PAIRS, P])
        stats = sb("stats", [P, SEQT, 6])
        meanvar = sb("meanvar", [P, SEQT, 2])
        rstd = sb("rstd", [P, SEQT])
        xn = sb("xn", [P, SEQT, D])
        xnT = sb("xnT", [P, SEQ])
        gelu = sb("gelu", [FW, 2, SEQ])
        hT = sb("hT", [FW, FCH, SEQ])

        ring = ctx.enter_context(nc.psum_tensor("ring", [P, 3, 1024], F32))
        tpose = ctx.enter_context(nc.psum_tensor("tpose", [P, 512], F32))
        yps = ctx.enter_context(nc.psum_tensor("yps", [P, 512], F32))

        names = ("cleared loaded ready weights_even weights_odd xs_in xsf_in v_even v_odd x_turned xT_copied "
                 "p_turned p_copied q_turned qT_copied k_turned kT_copied o_summed oT_copied scored "
                 "scores_taken exped y_made y_added q_made q_squared q_rotated k_made k_squared k_rotated v_made "
                 "v_copied squares_summed var_made rstd_made qk_roped probs_ready ropes_made w1_copied xn_made xn_turned "
                 "xnT_copied h_made gelu_made h_ready f_made x_done stood dve_own pool_own act_own").split()
        s = {n: ctx.enter_context(nc.semaphore("l_" + n)) for n in names}
        GROUPS = DEPTH * BATCH
        VPLACED = 4 * WT * 16
        XSHIFT = 3 * 16

        STEP = ("PT", "QT", "KT", "OT", "S", "Q", "K", "V")
        LAG = {"PT": 2, "QT": 1, "KT": 1, "OT": 2, "S": 1, "Q": 0, "K": 0, "V": 0}
        USES = [(kind, step) for step in range(3) for kind in STEP] + [("XN", 0)]
        USES += [(kind, 3) for kind in STEP] + [("H", c) for c in range(FCH)]
        FREED = {"PT": ("p_copied",), "QT": ("qT_copied",), "KT": ("kT_copied",), "OT": ("oT_copied",),
                 "S": ("scores_taken",), "Q": ("q_rotated",), "K": ("k_rotated",), "V": ("v_copied",),
                 "XN": ("xnT_copied",), "H": ("gelu_made", "h_ready")}
        assert len(USES) % 3 == 0

        def count(kind, step, g):
            if kind == "XN":
                n, last = g, GROUPS
            elif kind == "H":
                n, last = FCH * (g - 1) + step + 1, FCH * GROUPS
            else:
                n, last = SEQT * g + step - LAG[kind] + 1, SEQT * GROUPS
            return None if isinstance(g, int) and not 0 < n <= last else n

        def slot(kind, step):
            return USES.index((kind, step)) % 3

        def take(pe, kind, step, g):
            u = USES.index((kind, step)) - 3
            while not isinstance(g, int) or g + u // len(USES) >= 0:
                held = USES[u % len(USES)]
                before = count(*held, g + u // len(USES))
                if before is not None:
                    for name in FREED[held[0]]:
                        pe.wait_ge(s[name], before)
                    break
                u -= 3
            return ring[:, slot(kind, step), :]

        def live(t):
            return not isinstance(t, int) or 0 <= t < SEQT * GROUPS

        def weights_in(eng, g):
            layer = g // BATCH
            eng.wait_ge(s["weights_even"], 128 * (layer // 2 + 1))
            at_least(eng, s["weights_odd"], 128 * ((layer + 1) // 2))

        block = ctx.enter_context(nc.Block())

        @block.sync
        def _(sp):
            def load_layer(layer, parity):
                stand(sp, s["stood"])
                for dst, src in ((wqkv[:, parity, :], w["wqkv"]), (wo[:, parity, :, :], w["wo"]),
                                 (w1ring[:, parity, :], w["w1"]), (w2[:, parity, :, :], w["w2"]),
                                 (b1[:, parity, :], w["b1"]), (ln[:, parity, :], w["ln"]),
                                 (b2[:, parity, :], w["b2"]), (qkscale[:, parity, :, :], w["qk"])):
                    sp.dma_start(dst, src[layer]).then_inc(s["weights_odd" if parity else "weights_even"], 16)

            def shift_in(dst, g, signal):
                stand(sp, s["stood"])
                tiles = x[:, bass.ds(g % BATCH * SEQT, SEQT), :]
                before = x[:, bass.ds(g % BATCH * SEQT, SEQT - 1), :]
                sp.dma_start(dst[:, :, 0:D // 2], tiles[:, :, 0:D // 2]).then_inc(signal, 16)
                sp.dma_start(dst[1:P, :, D // 2:D], tiles[0:P - 1, :, D // 2:D]).then_inc(signal, 16)
                sp.dma_start(dst[0:1, 1:SEQT, D // 2:D], before[P - 1:P, :, D // 2:D]).then_inc(signal, 16)

            def body(g):
                for step in range(SEQT):
                    t = SEQT * g + step
                    if step == 1 and live(SEQT * (g - 1)):
                        sp.wait_ge(s["y_added"], SEQT * g)
                        stand(sp, s["stood"])
                        at_least(sp, s["xn_made"], g - 1)
                        shift_in(xsf, g - 1, s["xsf_in"])
                    if live(t):
                        placed = s["v_odd" if step % 2 else "v_even"]
                        sp.wait_ge(s["v_copied"], t + 1)
                        stand(sp, s["stood"])
                        at_least(sp, s["o_summed"], t - 1)
                        for hp in range(2):
                            for win in range(WT):
                                half = slice(hp * (INNER // 2), (hp + 1) * (INNER // 2))
                                at = (step % 2) * WT + win
                                now = v[W * win:W * win + W, step % 2, half]
                                before = v[W * win - W:W * win, step % 2, half] if win else v[P - W:P, 1 - step % 2, half]
                                sp.dma_start(vwin[64 * hp + W:64 * hp + 2 * W, at, :], now).then_inc(placed, 16)
                                sp.dma_start(vwin[64 * hp:64 * hp + W, at, :], before).then_inc(placed, 16)
                    if step == 3 and live(SEQT * (g + 1)):
                        at_least(sp, s["x_done"], g + 1 - BATCH + 1)
                        sp.wait_ge(s["x_turned"], SEQT * (g + 1))
                        shift_in(xs, g + 1, s["xs_in"])

            for dst, src in ((rope[:, :, :, :], w["rope"]), (ident[:, :], w["ident"])):
                sp.dma_start(dst, src).then_inc(s["loaded"], 16)
            sp.wait_ge(s["cleared"], 4)
            shift_in(xs, 0, s["xs_in"])
            load_layer(0, 0)
            load_layer(1, 1)
            for b in range(BATCH):
                body(b)

            def layer_groups(layer, next_parity):
                for b in range(BATCH):
                    body(BATCH * layer + b)
                    if b == 1 and next_parity is not None:
                        sp.wait_ge(s["x_done"], BATCH * layer)
                        load_layer(layer + 1, next_parity)

            with sp.Fori(0, (DEPTH - 2) // 2) as two:
                layer_groups(2 * two + 1, 0)
                layer_groups(2 * two + 2, 1)
            for b in range(BATCH):
                body(BATCH * (DEPTH - 1) + b)
            body(GROUPS)

        @block.gpsimd
        def _(pool):
            own = Tally(s["pool_own"])
            nc.gpsimd.memset(v[:, 1, :], 0.0).then_inc(s["cleared"], 1)
            nc.gpsimd.memset(kT[:, 1, :, P:P + W], 0.0).then_inc(s["cleared"], 1)
            nc.gpsimd.memset(xs[0:1, :, :], 0.0).then_inc(s["cleared"], 1)
            nc.gpsimd.memset(xsf[0:1, :, :], 0.0).then_inc(s["cleared"], 1)
            own.add(nc.gpsimd.memset(power[:, :], -0.5))
            own.add(nc.gpsimd.memset(eps[:, :], EPS))
            own.add(nc.gpsimd.memset(bias[:, :, :, :], 0.0))
            own.settle(pool)
            for first in range(2):
                for win in range(WT):
                    view = bias[W * win:W * win + W, first, :, :]
                    own.add(nc.gpsimd.affine_select(out=view, in_=view, compare_op=ALU.is_ge, fill=MASKED, base=0,
                                                    pattern=[[0, 8], [1, W2]], channel_multiplier=-1))
                    own.settle(pool)
                    own.add(nc.gpsimd.affine_select(out=view, in_=view, compare_op=ALU.is_ge, fill=MASKED, base=W,
                                                    pattern=[[0, 8], [-1, W2]], channel_multiplier=1))
                    own.settle(pool)
            own.add(nc.gpsimd.memset(bias[0:W, 1, :, 0:W], MASKED))
            own.settle(pool)
            pool.wait_ge(s["loaded"], 32)
            nc.gpsimd.tensor_copy(identb[:, :], ident[:, :]).then_inc(s["ready"], 1)
            own.close()

            def body(g):
                if live(SEQT * g):
                    weights_in(pool, g)
                    at_least(pool, s["k_rotated"], SEQT * (g - 1))
                    scales = qkscale[:, (g // BATCH) % 2, :, :]
                    for n in range(2):
                        scale = scales[:, n:n + 1, :].broadcast_to([P, SEQT * 2, DH])
                        nc.gpsimd.tensor_tensor(ropes[:, g % 2, n, :, :], rope[:, n, :, :], scale,
                                                ALU.mult).then_inc(s["ropes_made"], 1)
                for step in range(SEQT):
                    t = SEQT * g + step
                    if live(t):
                        for n, name in enumerate("qk"):
                            pool.wait_ge(s[name + "_rotated"], t + 1)
                            at_least(pool, s[name + "_turned"], t)
                            halves = [y.rearrange("p (h s e) -> p h s e", s=2, e=DH // 2)
                                      for y in (turned[:, n, 0, :], turned[:, n, 1, :], roped[:, n, :])]
                            for side in range(2):
                                own.add(nc.gpsimd.tensor_tensor(halves[2][:, :, side, :], halves[0][:, :, side, :],
                                                                halves[1][:, :, 1 - side, :], ALU.add))
                            pool.wait_ge(s["squares_summed"], 2 * t + n + 1)
                            sums = ss[:, n * HEADS:(n + 1) * HEADS]
                            at_least(pool, s["qk_roped"], 2 * t + n - 1)
                            own.add(nc.gpsimd.tensor_tensor(rnorm[:, n, :], sums, power[:, :], ALU.pow))
                            own.settle(pool)
                            norm = rnorm[:, n, :].unsqueeze(2).broadcast_to([P, HEADS, DH])
                            whole = roped[:, n, :].rearrange("p (h d) -> p h d", d=DH)
                            nc.gpsimd.tensor_tensor(whole, whole, norm, ALU.mult).then_inc(s["qk_roped"], 1)
                    if step == 2 and live(SEQT * (g - 1)):
                        pool.wait_ge(s["var_made"], g)
                        own.add(nc.gpsimd.tensor_tensor(rstd[:, :], meanvar[:, :, 1], eps[:, :], ALU.add))
                        own.settle(pool)
                        nc.gpsimd.tensor_tensor(rstd[:, :], rstd[:, :], power[:, 0:SEQT], ALU.pow
                                                ).then_inc(s["rstd_made"], 1)
                        at_least(pool, s["h_made"], FCH * (g - 1))
                        nc.gpsimd.tensor_copy(w1[:, :], w1ring[:, ((g - 1) // BATCH) % 2, :]
                                              ).then_inc(s["w1_copied"], 1)

            rounds(pool, 0, GROUPS, body, own, 6 * SEQT + 1)

        @block.scalar
        def _(act):
            own = Tally(s["act_own"])

            def body(g):
                if live(SEQT * g):
                    weights_in(act, g)
                for step in range(SEQT):
                    a, b, c = (SEQT * g + step - lag for lag in range(3))
                    pa, pb = step % 2, (step + 1) % 2
                    if live(a):
                        act.wait_ge(s["x_turned"], a + 1)
                        at_least(act, s["v_made"], a - 1)
                        nc.scalar.copy(xT[:, pa, :], tpose[:, 0:P]).then_inc(s["xT_copied"], 1)
                    if live(c):
                        act.wait_ge(s["p_turned"], c + 1)
                        at_least(act, s["o_summed"], c)
                        nc.scalar.copy(pT[:, :, :].rearrange("p a b -> p (a b)"),
                                       ring[:, slot("PT", step), :]).then_inc(s["p_copied"], 1)
                    if live(b):
                        act.wait_ge(s["q_turned"], b + 1)
                        at_least(act, s["scored"], b)
                        nc.scalar.copy(qT[:, :, :].rearrange("p a b -> p (a b)"),
                                       ring[:, slot("QT", step), :]).then_inc(s["qT_copied"], 1)
                        at_least(act, s["kT_copied"], b)
                        if isinstance(b, int) and b == 0:
                            act.wait_ge(s["cleared"], 4)
                        own.add(nc.scalar.copy(kT[:, pb, :, 0:W], kT[:, 1 - pb, :, P:P + W]))
                        act.wait_ge(s["k_turned"], b + 1)
                        own.settle(act)
                        nc.scalar.copy(kT[:, pb, :, W:W + P],
                                       ring[:, slot("KT", step), :].rearrange("p (a b) -> p a b", b=P)
                                       ).then_inc(s["kT_copied"], 1)
                    if live(c):
                        act.wait_ge(s["o_summed"], c + 1)
                        at_least(act, s["y_made"], c)
                        nc.scalar.copy(oT[:, :, :].rearrange("p a b -> p (a b)"),
                                       ring[:, slot("OT", step), :]).then_inc(s["oT_copied"], 1)
                    if live(b):
                        act.wait_ge(s["scores_taken"], b + 1)
                        flat = probs[:, pb, :, :].rearrange("p h k -> p (h k)")
                        nc.scalar.activation(flat, flat, ACT.Exp, scale=QK_SCALE).then_inc(s["exped"], 1)
                    if live(a):
                        for n, name in enumerate("qk"):
                            act.wait_ge(s[name + "_made"], a + 1)
                            at_least(act, s["squares_summed"], 2 * a + n)
                            nc.scalar.activation(squares[:, :], ring[:, slot(name.upper(), step), :],
                                                 ACT.Square).then_inc(s[name + "_squared"], 1)
                        act.wait_ge(s["v_made"], a + 1)
                        near, far = ("v_even", "v_odd") if pa else ("v_odd", "v_even")
                        at_least(act, s[near], (2 * g + (step + 1) // 2) * VPLACED)
                        at_least(act, s[far], (2 * g + step // 2) * VPLACED)
                        nc.scalar.copy(v[:, pa, :].rearrange("p (s h e) -> p h s e", s=2, e=DH),
                                       ring[:, slot("V", step), :].rearrange("p (h s e) -> p h s e", s=2, e=DH)
                                       ).then_inc(s["v_copied"], 1)
                    if step == 2 and live(SEQT * (g - 1)):
                        act.wait_ge(s["xn_turned"], g)
                        at_least(act, s["h_made"], FCH * (g - 1))
                        of = ln[:, ((g - 1) // BATCH) % 2, :]
                        nc.scalar.activation(xnT[:, :], ring[:, slot("XN", 0), 0:SEQ], ACT.Identity,
                                             scale=of[:, 0:1], bias=of[:, 1:2]).then_inc(s["xnT_copied"], 1)
                if live(SEQT * (g - 1)):
                    of = b1[:, ((g - 1) // BATCH) % 2, :]
                    for c in range(FCH):
                        n = FCH * (g - 1) + c
                        act.wait_ge(s["h_made"], n + 1)
                        at_least(act, s["h_ready"], FCH * (g - 1) if c < 2 else n - 1)
                        nc.scalar.activation(gelu[:, c % 2, :], ring[0:FW, slot("H", c), 0:SEQ], ACT.Gelu,
                                             bias=of[:, FCH + c:FCH + c + 1]).then_inc(s["gelu_made"], 1)

            rounds(act, 0, GROUPS, body, own, SEQT)

        @block.tensor
        def _(pe):
            def body(g):
                if live(SEQT * g):
                    weights_in(pe, g)
                    pe.wait_ge(s["xs_in"], XSHIFT * (g + 1))
                for step in range(SEQT):
                    a, b, c = (SEQT * g + step - lag for lag in range(3))
                    pa, pb = step % 2, (step + 1) % 2
                    if live(a):
                        at_least(pe, s["xT_copied"], a)
                        nc.tensor.transpose(tpose[:, 0:P], xs[:, step, :], ident[:, :]).then_inc(s["x_turned"], 1)
                    if live(c):
                        pe.wait_ge(s["probs_ready"], c + 1)
                        out = take(pe, "PT", step, g)
                        for pair in range(PAIRS):
                            last = nc.tensor.transpose(
                                out[:, pair * P:(pair + 1) * P],
                                probs[:, pa, 2 * pair:2 * pair + 2, :].rearrange("p h k -> p (h k)"), ident[:, :])
                        last.then_inc(s["p_turned"], 1)
                    if live(b):
                        for n, (name, kind) in enumerate((("q_turned", "QT"), ("k_turned", "KT"))):
                            pe.wait_ge(s["qk_roped"], 2 * b + n + 1)
                            out = take(pe, kind, step, g)
                            for pair in range(PAIRS):
                                last = nc.tensor.transpose(out[:, pair * P:(pair + 1) * P],
                                                           roped[:, n, pair * P:(pair + 1) * P], ident[:, :])
                            last.then_inc(s[name], 1)
                    if live(c):
                        pe.wait_ge(s["p_copied"], c + 1)
                        even = step % 2 == 0
                        pe.wait_ge(s["v_even" if even else "v_odd"], (2 * g + (step - 2) // 2 + 1) * VPLACED)
                        out = take(pe, "OT", step, g)
                        stand(pe, s["stood"])
                        for pair in range(PAIRS):
                            for hp in range(2):
                                keys = slice(64 * hp, 64 * hp + 64)
                                for win in range(WT):
                                    at = pair * P + W * win
                                    last = nc.tensor.matmul(
                                        out[keys, at:at + W], vwin[keys, pa * WT + win, pair * DH:(pair + 1) * DH],
                                        pT[keys, pair, W * win:W * win + W], start=True, stop=True)
                        last.then_inc(s["o_summed"], 1)
                    if live(b):
                        pe.wait_ge(s["qT_copied"], b + 1)
                        pe.wait_ge(s["kT_copied"], b + 1)
                        out = take(pe, "S", step, g)
                        for half in range(2):
                            nc.tensor.matmul(out[:, half * 512:(half + 1) * 512], identb[:, :],
                                             bias[:, 1 if step == 1 else 0, :, :].rearrange("p h k -> p (h k)"),
                                             start=True, stop=False, skip_group_check=True)
                        for pair in range(PAIRS):
                            for hp in range(2):
                                dims = slice(64 * hp, 64 * hp + 64)
                                for win in range(WT):
                                    at = hp * 512 + pair * W2
                                    last = nc.tensor.matmul(
                                        out[W * win:W * win + W, at:at + W2], qT[dims, pair, W * win:W * win + W],
                                        kT[dims, pb, pair, W * win:W * win + W2],
                                        start=False, stop=True, skip_group_check=True)
                        last.then_inc(s["scored"], 1)
                    if live(c):
                        pe.wait_ge(s["oT_copied"], c + 1)
                        at_least(pe, s["y_added"], c)
                        at_least(pe, s["x_done"], g - 1)
                        for pair in range(PAIRS):
                            last = nc.tensor.matmul(yps[:, 0:D], oT[:, pair, :], wo[:, (c // (SEQT * BATCH)) % 2, pair, :],
                                                    start=pair == 0, stop=pair == PAIRS - 1)
                        last.then_inc(s["y_made"], 1)
                    if live(a):
                        pe.wait_ge(s["xT_copied"], a + 1)
                        for n, name in enumerate("qkv"):
                            out = take(pe, name.upper(), step, g)
                            for half in range(2):
                                last = nc.tensor.matmul(
                                    out[:, half * 512:(half + 1) * 512], xT[:, pa, :],
                                    wqkv[:, (g // BATCH) % 2, bass.ds(n * INNER + half * 512, 512)],
                                    start=True, stop=True)
                            last.then_inc(s[name + "_made"], 1)
                    if step == 2 and live(SEQT * (g - 1)):
                        pe.wait_ge(s["xn_made"], g)
                        out = take(pe, "XN", 0, g)
                        for tile in range(SEQT):
                            last = nc.tensor.transpose(out[:, tile * P:(tile + 1) * P], xn[:, tile, :], ident[:, :])
                        last.then_inc(s["xn_turned"], 1)
                if live(SEQT * (g - 1)):
                    pe.wait_ge(s["xnT_copied"], g)
                    pe.wait_ge(s["w1_copied"], g)
                    for c in range(FCH):
                        out = take(pe, "H", c, g)
                        for n, part in enumerate((FCH + c, c)):
                            last = nc.tensor.matmul(out[0:FW, n * 512:(n + 1) * 512], w1[:, part * FW:(part + 1) * FW],
                                                    xnT[:, :], start=True, stop=True)
                        last.then_inc(s["h_made"], 1)
                    pe.wait_ge(s["h_ready"], FCH * g)
                    pe.wait_ge(s["y_added"], min(SEQT * g + 2, SEQT * GROUPS) if isinstance(g, int) else SEQT * g + 2)
                    for tile in range(SEQT):
                        for c in range(FCH):
                            last = nc.tensor.matmul(yps[:, tile * D:(tile + 1) * D], hT[:, c, tile * P:(tile + 1) * P],
                                                    w2[:, ((g - 1) // BATCH) % 2, c, :], start=c == 0, stop=c == FCH - 1)
                    last.then_inc(s["f_made"], 1)

            pe.wait_ge(s["loaded"], 32)
            pe.wait_ge(s["ready"], 1)
            body(0)
            rounds(pe, 1, GROUPS, body)

        @block.vector
        def _(dve):
            own = Tally(s["dve_own"])

            def body(g):
                if live(SEQT * g):
                    weights_in(dve, g)
                    dve.wait_ge(s["ropes_made"], 2 * (g + 1))
                for step in range(SEQT):
                    a, b, c = (SEQT * g + step - lag for lag in range(3))
                    pa, pb = step % 2, (step + 1) % 2
                    if live(b):
                        dve.wait_ge(s["scored"], b + 1)
                        scores = ring[:, slot("S", step), :].rearrange("p (h k) -> p h k", k=W2)
                        own.add(nc.vector.tensor_reduce(smax[:, :], scores, AX.X, ALU.max))
                        at_least(dve, s["p_turned"], b - 1)
                        own.settle(dve)
                        nc.vector.tensor_tensor(
                            probs[:, pb, :, :].rearrange("p (h s) k -> p s h k", s=2),
                            scores.rearrange("p (s h) k -> p s h k", s=2),
                            smax[:, :].rearrange("p (s h) -> p s h", s=2).unsqueeze(3).broadcast_to([P, 2, PAIRS, W2]),
                            ALU.subtract).then_inc(s["scores_taken"], 1)
                    if live(c):
                        dve.wait_ge(s["y_made"], c + 1)
                        row = x[:, c % TILES, :]
                        nc.vector.tensor_tensor(row, yps[:, 0:D], row, ALU.add).then_inc(s["y_added"], 1)
                    if live(a):
                        for n, name in enumerate("qk"):
                            dve.wait_ge(s[name + "_squared"], a + 1)
                            at_least(dve, s["qk_roped"], 2 * a - 1 + n)
                            heads = ring[:, slot(name.upper(), step), :].rearrange("p (h d) -> p h d", d=DH)
                            for part in range(2):
                                table = ropes[:, g % 2, n, 2 * step + part:2 * step + part + 1, :].broadcast_to([P, HEADS, DH])
                                ins = nc.vector.tensor_tensor(
                                    turned[:, n, part, :].rearrange("p (h d) -> p h d", d=DH), heads, table, ALU.mult)
                            ins.then_inc(s[name + "_rotated"], 1)
                            at_least(dve, s["qk_roped"], 2 * a - 1 + n)
                            sums = ss[:, n * HEADS:(n + 1) * HEADS]
                            own.add(nc.vector.tensor_reduce(sums, squares[:, :].rearrange("p (h d) -> p h d", d=DH),
                                                            AX.X, ALU.add))
                            own.settle(dve)
                            nc.vector.tensor_scalar(sums, sums, NORM_FLOOR, None, ALU.max
                                                    ).then_inc(s["squares_summed"], 1)
                    if live(b):
                        dve.wait_ge(s["exped"], b + 1)
                        own.add(nc.vector.tensor_reduce(rsum[:, 0, :], probs[:, pb, :, :], AX.X, ALU.add))
                        own.settle(dve)
                        own.add(nc.vector.reciprocal(rsum[:, 1, :], rsum[:, 0, :]))
                        own.settle(dve)
                        nc.vector.tensor_tensor(probs[:, pb, :, :], probs[:, pb, :, :],
                                                rsum[:, 1, :].unsqueeze(2).broadcast_to([P, HEADS, W2]),
                                                ALU.mult).then_inc(s["probs_ready"], 1)
                    if step == 2 and live(SEQT * (g - 1)):
                        dve.wait_ge(s["xsf_in"], XSHIFT * g)
                        at_least(dve, s["xn_turned"], g - 1)
                        for tile in range(SEQT):
                            own.add(nc.vector.bn_stats(stats[:, tile, :], xsf[:, tile, :]))
                        own.settle(dve)
                        tiles = x[:, bass.ds((g - 1) % BATCH * SEQT, SEQT), :]
                        lp = ((g - 1) // BATCH) % 2
                        own.add(nc.vector.tensor_tensor(tiles, tiles,
                                                        b2[:, lp, :].unsqueeze(1).broadcast_to([P, SEQT, D]), ALU.add))
                        for tile in range(SEQT):
                            ins = nc.vector.bn_aggr(meanvar[:, tile, :], stats[:, tile, :])
                        ins.then_inc(s["var_made"], 1)
                        dve.wait_ge(s["rstd_made"], g)
                        for tile in range(SEQT):
                            ins = nc.vector.tensor_scalar(xn[:, tile, :], xsf[:, tile, :], meanvar[:, tile, 0:1],
                                                          rstd[:, tile:tile + 1], ALU.subtract, ALU.mult)
                        ins.then_inc(s["xn_made"], 1)
                if live(SEQT * (g - 1)):
                    lp = ((g - 1) // BATCH) % 2
                    at_least(dve, s["f_made"], g - 1)
                    for c in range(FCH):
                        dve.wait_ge(s["gelu_made"], FCH * (g - 1) + c + 1)
                        nc.vector.scalar_tensor_tensor(hT[:, c, :], ring[0:FW, slot("H", c), 512:1024],
                                                       b1[:, lp, c:c + 1], gelu[:, c % 2, :], ALU.add,
                                                       ALU.mult).then_inc(s["h_ready"], 1)
                    tiles = x[:, bass.ds((g - 1) % BATCH * SEQT, SEQT), :]
                    own.settle(dve)
                    dve.wait_ge(s["f_made"], g)
                    nc.vector.tensor_tensor(tiles, yps[:, :].rearrange("p (t d) -> p t d", d=D), tiles,
                                            ALU.add).then_inc(s["x_done"], 1)

            rounds(dve, 0, GROUPS, body, own, 6 * SEQT + 1)


def layer_norm_tiles(nc, src, dst, name):
    with ExitStack() as ctx:
        stats = ctx.enter_context(nc.sbuf_tensor(name + "_stats", [P, TILES, 6], F32))
        meanvar = ctx.enter_context(nc.sbuf_tensor(name + "_meanvar", [P, TILES, 2], F32))
        rstd = ctx.enter_context(nc.sbuf_tensor(name + "_rstd", [P, TILES], F32))
        power = ctx.enter_context(nc.sbuf_tensor(name + "_power", [P, TILES], F32))
        stats_made, var_made, var_eps, power_made, rstd_made, normed = (
            ctx.enter_context(nc.semaphore(f"{name}_{n}"))
            for n in ("stats_made", "var_made", "var_eps", "power_made", "rstd_made", "normed"))
        with nc.Block() as block:
            @block.vector
            def _(dve):
                for t in range(TILES):
                    nc.vector.bn_stats(stats[:, t, :], src[:, t, :]).then_inc(stats_made, 1)
                dve.wait_ge(stats_made, TILES)
                for t in range(TILES):
                    nc.vector.bn_aggr(meanvar[:, t, :], stats[:, t, :]).then_inc(var_made, 1)
                dve.wait_ge(var_made, TILES)
                nc.vector.tensor_scalar(rstd[:, :], meanvar[:, :, 1], EPS, None, ALU.add).then_inc(var_eps, 1)
                dve.wait_ge(rstd_made, 1)
                for t in range(TILES):
                    nc.vector.tensor_scalar(dst[:, t, :], src[:, t, :], meanvar[:, t, 0:1], rstd[:, t:t + 1],
                                            ALU.subtract, ALU.mult).then_inc(normed, 1)
                dve.wait_ge(normed, TILES)

            @block.gpsimd
            def _(pool):
                nc.gpsimd.memset(power[:, :], -0.5).then_inc(power_made, 1)
                pool.wait_ge(power_made, 1)
                pool.wait_ge(var_eps, 1)
                nc.gpsimd.tensor_tensor(rstd[:, :], rstd[:, :], power[:, :], ALU.pow).then_inc(rstd_made, 1)


def relative_attention(nc, x, w, scratch):
    with ExitStack() as ctx:
        def sb(name, shape, dt=F32):
            return ctx.enter_context(nc.sbuf_tensor(name, shape, dt))

        def sem(name):
            return ctx.enter_context(nc.semaphore("a_" + name))

        S = SEQ
        EDGE = P + 1
        HEADS_ALL = BATCH * H0
        STEPS = S // P
        consts = sb("consts", [P, 2, S])
        fcols = sb("fcols", [P, 2, S + 1])
        mask = sb("mask", [P, 2 * EDGE])
        ident = sb("ident_a", [P, P])
        wproj = sb("wproj", [P, 4, D])
        cols = sb("cols", [P, 8])
        rows = sb("rows", [P, 2, D])
        attn = sb("attn", [P, TILES, D])
        vaug = sb("vaug", [P, TILES, H0, DP + 1])

        with ExitStack() as first:
            def sb1(name, shape):
                return first.enter_context(nc.sbuf_tensor(name, shape, F32))

            def sem1(name):
                return first.enter_context(nc.semaphore("p_" + name))

            qvT, quT, kTs = sb1("qvT", [P, TILES * P + 1]), sb1("quT", [P, TILES * P]), sb1("kTs", [P, TILES * P])
            xnT = sb1("xnT_a", [P, TILES * P])
            bps = sb1("bps", [P, S])
            layer_norm_tiles(nc, x, attn, "norm1")
            ps = first.enter_context(nc.psum_tensor("ps_a", [P, 8, 512], F32))
            loaded, turned, copied, biases, q_made, k_made, v_made, q_read, k_read, v_read, filled, stored = (
                sem1(n) for n in ("loaded turned copied biases q_made k_made v_made q_read k_read v_read filled "
                                  "stored").split())
            with nc.Block() as block:
                @block.sync
                def _(sp):
                    for dst, src in ((consts[:, :, :], w["turns"]), (fcols[:, :, :], w["fcols"]), (mask[:, :], w["mask"]),
                                     (ident[:, :], w["ident"]), (wproj[:, :, :], w["wproj"]), (cols[:, :], w["cols"]),
                                     (rows[:, :, :], w["rows"])):
                        sp.dma_start(dst, src).then_inc(loaded, 16)
                    sp.wait_ge(q_read, 2 * BATCH)
                    sp.wait_ge(filled, 3)
                    sp.dma_start(scratch["qv"], qvT[:, :]).then_inc(stored, 16)
                    sp.dma_start(scratch["qu"], quT[:, :]).then_inc(stored, 16)
                    sp.dma_start(scratch["bp"], bps[:, :]).then_inc(stored, 16)
                    sp.wait_ge(k_read, BATCH)
                    sp.dma_start(scratch["k"], kTs[:, :]).then_inc(stored, 16)
                    sp.wait_ge(stored, 4 * 16)

                @block.tensor
                def _(pe):
                    pe.wait_ge(loaded, 7 * 16)
                    for t in range(TILES):
                        bank = t // 4
                        nc.tensor.transpose(ps[:, bank, (t % 4) * P:(t % 4 + 1) * P], attn[:, t, :],
                                            ident[:, :]).then_inc(turned, 1)
                    for b in range(BATCH):
                        pe.wait_ge(copied, b + 1)
                        nc.tensor.matmul(ps[:, 4 + b % 2, :], wproj[:, 0, :], xnT[:, b * S:(b + 1) * S],
                                         start=True, stop=True).then_inc(q_made, 1) if b < 2 else None
                        if b < 2:
                            nc.tensor.matmul(ps[:, 6 + b, :], wproj[:, 1, :], xnT[:, b * S:(b + 1) * S],
                                             start=True, stop=True).then_inc(k_made, 1)
                    for b in range(2, BATCH):
                        pe.wait_ge(q_read, 2 * (b - 1))
                        nc.tensor.matmul(ps[:, 4 + b % 2, :], wproj[:, 0, :], xnT[:, b * S:(b + 1) * S],
                                         start=True, stop=True).then_inc(q_made, 1)
                        pe.wait_ge(k_read, b - 1)
                        nc.tensor.matmul(ps[:, 6 + b % 2, :], wproj[:, 1, :], xnT[:, b * S:(b + 1) * S],
                                         start=True, stop=True).then_inc(k_made, 1)
                    for t in range(TILES):
                        nc.tensor.matmul(ps[:, t // 4, (t % 4) * D:(t % 4 + 1) * D], xnT[:, t * P:(t + 1) * P],
                                         wproj[:, 2, :], start=True, stop=True).then_inc(v_made, 1)

                @block.scalar
                def _(act):
                    for b in range(BATCH):
                        act.wait_ge(turned, 4 * (b + 1))
                        nc.scalar.copy(xnT[:, b * S:(b + 1) * S], ps[:, b, :]).then_inc(copied, 1)
                    act.wait_ge(biases, 2)
                    for b in range(BATCH):
                        act.wait_ge(q_made, b + 1)
                        for dst, bias in ((qvT, 7), (quT, 6)):
                            nc.scalar.activation(dst[:, b * S:(b + 1) * S], ps[:, 4 + b % 2, :], ACT.Identity,
                                                 bias=cols[:, bias:bias + 1]).then_inc(q_read, 1)

                @block.vector
                def _(dve):
                    dve.wait_ge(loaded, 7 * 16)
                    nc.vector.tensor_tensor(cols[:, 6:7], cols[:, 0:1], cols[:, 2:3], ALU.add).then_inc(biases, 1)
                    nc.vector.tensor_tensor(cols[:, 7:8], cols[:, 0:1], cols[:, 3:4], ALU.add).then_inc(biases, 1)
                    nc.vector.memset(qvT[:, TILES * P:TILES * P + 1], 0.0).then_inc(filled, 1)
                    nc.vector.memset(vaug[:, :, :, DP:DP + 1], 1.0).then_inc(filled, 1)
                    nc.vector.tensor_copy(bps[:, :], cols[:, 4:5].broadcast_to([P, S])).then_inc(filled, 1)
                    for b in range(BATCH):
                        dve.wait_ge(k_made, b + 1)
                        nc.vector.tensor_scalar(kTs[:, b * S:(b + 1) * S], ps[:, 6 + b % 2, :], cols[:, 1:2], None,
                                                ALU.add).then_inc(k_read, 1)
                    for b in range(BATCH):
                        dve.wait_ge(v_made, 4 * (b + 1))
                        for t in range(4 * b, 4 * b + 4):
                            nc.vector.tensor_tensor(
                                vaug[:, t, :, 0:DP],
                                ps[:, b, (t % 4) * D:(t % 4 + 1) * D].rearrange("p (h d) -> p h d", d=DP),
                                rows[:, 0, :].rearrange("p (h d) -> p h d", d=DP), ALU.add).then_inc(v_read, 1)
                    dve.wait_ge(v_read, TILES)

        with ExitStack() as second:
            def sb2(name, shape):
                return second.enter_context(nc.sbuf_tensor(name, shape, F32))

            below = sb2("below", [2 * DP, 2, S])
            above = sb2("above", [2 * DP, 2, S])
            keys = sb2("keys", [2 * DP, 2, S])
            keys0 = sb2("keys0", [2 * DP, 2, S])
            wpT = sb2("wpT", [DP, 2, 2, D])
            qpart = sb2("qpart", [P, 2, S])
            qrot = sb2("qrot", [P, 2, S + 1])
            edge2 = sb2("edge2", [P, 2, 2 * EDGE])
            edge = sb2("edge", [P, 2, EDGE])
            top = sb2("top", [P, 2])
            shift = sb2("shift", [P, 2])
            probs = sb2("probs_a", [P, 2, S])
            pT = sb2("pT_a", [P, 2, STEPS, S])
            vhead = sb2("vhead", [P, 2, STEPS, DP + 1])
            oT = sb2("oT_a", [P, S])
            inv = sb2("inv", [P, STEPS])
            ps = second.enter_context(nc.psum_tensor("ps_b", [P, 8, 512], F32))
            names = ("heads_in0 heads_in1 zeroed g_made g_turned qrot_made edge_made edge_masked edge_summed scored "
                     "topped exped p_turned p_copied vhead_made o_summed o_copied o_turned o_done stood dve_own").split()
            s = {n: sem(n) for n in names}
            LOADS = 8 * 16
            N = HEADS_ALL

            def live(n):
                return not isinstance(n, int) or 0 <= n < N

            def live_step(m):
                return not isinstance(m, int) or 0 <= m < STEPS * N

            with nc.Block() as block:
                @block.sync
                def _(sp):
                    def load(n, par):
                        b, h = n % BATCH, n // BATCH
                        of = bass.ds(h * DP, DP)
                        here, ahead = bass.ds(b * S, S), bass.ds(b * S + 1, S)
                        at_least(sp, s["scored"], STEPS * (n - 1))
                        stand(sp, s["stood"])
                        for dst, src in ((below[0:DP, par, :], scratch["qv"][of, here]),
                                         (below[DP:2 * DP, par, :], scratch["qu"][of, here]),
                                         (above[0:DP, par, :], scratch["qv"][of, ahead]),
                                         (above[DP:2 * DP, par, :], scratch["qu"][of, here]),
                                         (keys[0:DP, par, :], scratch["bp"][of, :]),
                                         (keys[DP:2 * DP, par, :], scratch["k"][of, here]),
                                         (keys0[DP:2 * DP, par, :], scratch["k"][of, here]),
                                         (wpT[:, par, :, :], w["wpT"][h])):
                            sp.dma_start(dst, src).then_inc(s[f"heads_in{par}"], 16)
                    sp.wait_ge(s["zeroed"], 3)
                    load(0, 0)
                    load(1, 1)
                    with sp.Fori(1, N // 2) as two:
                        load(2 * two, 0)
                        load(2 * two + 1, 1)

                def steps(body):
                    def round_(two):
                        for par in range(2):
                            n = 2 * two + par
                            for it in range(STEPS):
                                body(n, par, it, STEPS * n + it)
                    return round_

                def two_rounds(eng, body, own=None, each=0):
                    rounds(eng, 0, N // 2 - 1, steps(body), own, each)
                    if own is not None:
                        own.close()
                    steps(body)(N // 2)

                @block.tensor
                def _(pe):
                    def turn(n, par):
                        pe.wait_ge(s[f"heads_in{par}"], LOADS * (n // 2 + 1))
                        at_least(pe, s["g_turned"], n)
                        at_least(pe, s["o_copied"], n - 1)
                        at_least(pe, s["o_done"], n - 2)
                        for half in range(2):
                            last = nc.tensor.matmul(ps[:, 4 + half, :], wpT[:, par, half, :], below[0:DP, par, :],
                                                    start=True, stop=True)
                        last.then_inc(s["g_made"], 1)

                    def edge_block(n, par, it, m):
                        if it == 0:
                            pe.wait_ge(s["qrot_made"], n + 1)
                        at_least(pe, s["edge_masked"], m - 1)
                        r = it * P
                        bank = ps[:, 2 + m_par(it), :]
                        for side, q, first in ((0, below, r), (1, above, r + 1)):
                            out = bank[:, side * EDGE:(side + 1) * EDGE]
                            nc.tensor.matmul(out, q[0:DP, par, r:r + P], keys[0:DP, par, 0:EDGE], start=True, stop=False)
                            last = nc.tensor.matmul(out, qrot[:, par, first:first + P], fcols[:, side, r:r + EDGE],
                                                    start=False, stop=True)
                        last.then_inc(s["edge_made"], 1)

                    def m_par(it):
                        return it % 2

                    def body(n, par, it, m):
                        if live(n):
                            at_least(pe, s["exped"], m - 1)
                            bank = ps[:, it % 2, :]
                            r = it * P
                            right = min(r + EDGE, S)
                            if r:
                                nc.tensor.matmul(bank[:, 0:r], below[:, par, r:r + P], keys[:, par, 0:r],
                                                 start=True, stop=False)
                                nc.tensor.matmul(bank[:, 0:r], qrot[:, par, r:r + P], fcols[:, 0, 0:r],
                                                 start=False, stop=True)
                            last = nc.tensor.matmul(bank[:, r:right], below[:, par, r:r + P], keys0[:, par, r:right],
                                                    start=True, stop=True)
                            if right < S:
                                nc.tensor.matmul(bank[:, right:S], above[:, par, r:r + P], keys[:, par, right:S],
                                                 start=True, stop=False)
                                last = nc.tensor.matmul(bank[:, right:S], qrot[:, par, r + 1:r + 1 + P],
                                                        fcols[:, 1, right:S], start=False, stop=True)
                            last.then_inc(s["scored"], 1)
                        if live_step(m - 1):
                            pe.wait_ge(s["exped"], m)
                            at_least(pe, s["p_copied"], m - 2)
                            for jt in range(STEPS):
                                last = nc.tensor.transpose(ps[:, 6 + (it + 1) % 2, jt * P:(jt + 1) * P],
                                                           probs[:, (it + 1) % 2, jt * P:(jt + 1) * P], ident[:, :])
                            last.then_inc(s["p_turned"], 1)
                        if it == 1 and live(n - 1):
                            pe.wait_ge(s["vhead_made"], n)
                            pe.wait_ge(s["p_copied"], STEPS * n)
                            pe.wait_ge(s["g_turned"], min(n + 1, N) if isinstance(n, int) else n + 1)
                            at_least(pe, s["o_copied"], n - 1)
                            for jt in range(STEPS):
                                last = nc.tensor.matmul(ps[0:DP + 1, 4, :], vhead[:, 1 - par, jt, :],
                                                        pT[:, 1 - par, jt, :], start=jt == 0, stop=jt == STEPS - 1)
                            last.then_inc(s["o_summed"], 1)
                        if it == 2 and live(n) and live(n + 1):
                            turn(n + 1, 1 - par)
                        if it == 3 and live(n - 1):
                            pe.wait_ge(s["o_copied"], n)
                            pe.wait_ge(s["g_turned"], min(n + 2, N) if isinstance(n, int) else n + 2)
                            at_least(pe, s["o_done"], n - 1)
                            for jt in range(STEPS):
                                last = nc.tensor.transpose(ps[:, 5, jt * P:(jt + 1) * P], oT[:, jt * P:(jt + 1) * P],
                                                           ident[:, :])
                            last.then_inc(s["o_turned"], 1)
                        nxt = (n, par, it + 1) if it + 1 < STEPS else (n + 1, 1 - par, 0)
                        if live(n) and live(nxt[0]):
                            edge_block(*nxt, m + 1)

                    pe.wait_ge(s["zeroed"], 3)
                    turn(0, 0)
                    edge_block(0, 0, 0, 0)
                    two_rounds(pe, body)

                @block.vector
                def _(dve):
                    own = Tally(s["dve_own"])

                    def turn(n, par):
                        dve.wait_ge(s["g_made"], n + 1)
                        at_least(dve, s["qrot_made"], n)
                        for half in range(2):
                            ins = nc.vector.tensor_tensor(qpart[:, half, :], ps[:, 4 + half, :], consts[:, half, :], ALU.mult)
                        ins.then_inc(s["g_turned"], 1)

                    def mask_edge(it, m):
                        dve.wait_ge(s["edge_made"], m + 1)
                        at_least(dve, s["edge_summed"], m - 1)
                        nc.vector.tensor_tensor(edge2[:, it % 2, :], ps[:, 2 + it % 2, 0:2 * EDGE], mask[:, :],
                                                ALU.mult).then_inc(s["edge_masked"], 1)

                    def body(n, par, it, m):
                        if live(n):
                            r = it * P
                            right = min(r + EDGE, S)
                            bank = ps[:, it % 2, :]
                            dve.wait_ge(s["scored"], m + 1)
                            dve.wait_ge(s["edge_summed"], m + 1)
                            own.add(nc.vector.tensor_tensor(bank[:, r:right], bank[:, r:right], edge[:, it % 2, 0:right - r],
                                                            ALU.add))
                            own.settle(dve)
                            own.add(nc.vector.tensor_reduce(top[:, it % 2:it % 2 + 1], bank, AX.X, ALU.max))
                            own.settle(dve)
                            at_least(dve, s["exped"], m - 1)
                            nc.vector.tensor_scalar(shift[:, it % 2:it % 2 + 1], top[:, it % 2:it % 2 + 1], -SCALE0, None,
                                                    ALU.mult).then_inc(s["topped"], 1)
                        if it == 2 and live(n) and live(n + 1):
                            turn(n + 1, 1 - par)
                        if live(n) and (it + 1 < STEPS or live(n + 1)):
                            mask_edge(it + 1, m + 1)
                        if it == 3 and live(n - 1):
                            b, h = (n - 1) % BATCH, (n - 1) // BATCH
                            dve.wait_ge(s["o_turned"], n)
                            o = ps[:, 5, :].rearrange("p (t d) -> p t d", d=P)
                            own.add(nc.vector.reciprocal(inv[:, :], o[:, :, DP]))
                            own.settle(dve)
                            nc.vector.tensor_tensor(attn[:, bass.ds(b * STEPS, STEPS), bass.ds(h * DP, DP)],
                                                    o[:, :, 0:DP], inv[:, :].unsqueeze(2).broadcast_to([P, STEPS, DP]),
                                                    ALU.mult).then_inc(s["o_done"], 1)

                    nc.vector.memset(keys0[0:DP, :, :], 0.0).then_inc(s["zeroed"], 1)
                    nc.vector.memset(qrot[:, :, S:S + 1], 0.0).then_inc(s["zeroed"], 1)
                    nc.vector.memset(oT[:, :], 0.0).then_inc(s["zeroed"], 1)
                    turn(0, 0)
                    mask_edge(0, 0)
                    two_rounds(dve, body, own, 2 * (2 * STEPS + 1))
                    dve.wait_ge(s["o_done"], N)

                @block.gpsimd
                def _(pool):
                    def turn(n, par):
                        pool.wait_ge(s["g_turned"], n + 1)
                        at_least(pool, s["scored"], STEPS * (n - 1))
                        nc.gpsimd.tensor_tensor(qrot[:, par, 0:S], qpart[:, 0, :], qpart[:, 1, :],
                                                ALU.add).then_inc(s["qrot_made"], 1)

                    def sum_edge(it, m):
                        pool.wait_ge(s["edge_masked"], m + 1)
                        at_least(pool, s["topped"], m - 1)
                        nc.gpsimd.tensor_tensor(edge[:, it % 2, :], edge2[:, it % 2, 0:EDGE], edge2[:, it % 2, EDGE:2 * EDGE],
                                                ALU.add).then_inc(s["edge_summed"], 1)

                    def body(n, par, it, m):
                        if it == 2 and live(n) and live(n + 1):
                            turn(n + 1, 1 - par)
                        if live(n) and (it + 1 < STEPS or live(n + 1)):
                            sum_edge(it + 1, m + 1)
                        if it == 0 and live(n):
                            b, h = n % BATCH, n // BATCH
                            at_least(pool, s["o_summed"], n - 1)
                            nc.gpsimd.tensor_copy(vhead[:, par, :, :], vaug[:, bass.ds(b * STEPS, STEPS), h, :]
                                                  ).then_inc(s["vhead_made"], 1)

                    turn(0, 0)
                    sum_edge(0, 0)
                    two_rounds(pool, body)

                @block.scalar
                def _(act):
                    def body(n, par, it, m):
                        if live(n):
                            act.wait_ge(s["topped"], m + 1)
                            at_least(act, s["p_turned"], m - 1)
                            nc.scalar.activation(probs[:, it % 2, :], ps[:, it % 2, :], ACT.Exp, scale=SCALE0,
                                                 bias=shift[:, it % 2:it % 2 + 1]).then_inc(s["exped"], 1)
                        if (live(n) and it) or live(n - 1) and it == 0:
                            hp, bt = (par, it - 1) if it else (1 - par, STEPS - 1)
                            act.wait_ge(s["p_turned"], m)
                            if it == 1:
                                at_least(act, s["o_summed"], n - 1)
                            nc.scalar.copy(pT[:, hp, :, bt * P:(bt + 1) * P],
                                           ps[:, 6 + bt % 2, :].rearrange("p (j c) -> p j c", c=P)
                                           ).then_inc(s["p_copied"], 1)
                        if it == 1 and live(n - 1):
                            act.wait_ge(s["o_summed"], n)
                            act.wait_ge(s["zeroed"], 3)
                            at_least(act, s["o_turned"], n - 1)
                            nc.scalar.copy(oT[0:DP + 1, :], ps[0:DP + 1, 4, :]).then_inc(s["o_copied"], 1)
                    two_rounds(act, body)

        with ExitStack() as third:
            aT = third.enter_context(nc.sbuf_tensor("aT", [P, TILES, P], F32))
            ps = third.enter_context(nc.psum_tensor("ps_c", [P, 8, 512], F32))
            turned, copied, projected, added = (sem("c_" + n) for n in ("turned", "copied", "projected", "added"))
            with nc.Block() as block:
                @block.tensor
                def _(pe):
                    for t in range(TILES):
                        nc.tensor.transpose(ps[:, t // 4, (t % 4) * P:(t % 4 + 1) * P], attn[:, t, :],
                                            ident[:, :]).then_inc(turned, 1)
                    for t in range(TILES):
                        pe.wait_ge(copied, t // 4 + 1)
                        nc.tensor.matmul(ps[:, 4 + t // 4, (t % 4) * D:(t % 4 + 1) * D], aT[:, t, :], wproj[:, 3, :],
                                         start=True, stop=True).then_inc(projected, 1)

                @block.scalar
                def _(act):
                    for b in range(BATCH):
                        act.wait_ge(turned, 4 * (b + 1))
                        nc.scalar.copy(aT[:, 4 * b:4 * b + 4, :].rearrange("p t c -> p (t c)"),
                                       ps[:, b, :]).then_inc(copied, 1)

                @block.vector
                def _(dve):
                    tiles = x[:, :, :]
                    nc.vector.tensor_tensor(tiles, tiles, rows[:, 1:2, :].broadcast_to([P, TILES, D]),
                                            ALU.add).then_inc(added, 1)
                    dve.wait_ge(added, 1)
                    for b in range(BATCH):
                        dve.wait_ge(projected, 4 * (b + 1))
                        tiles = x[:, 4 * b:4 * b + 4, :].rearrange("p t d -> p (t d)")
                        nc.vector.tensor_tensor(tiles, ps[:, 4 + b, :], tiles, ALU.add).then_inc(added, 1)
                    dve.wait_ge(added, 1 + BATCH)


def whole_kernel(nc, x_in, out, attention, layers):
    with ExitStack() as ctx:
        x1 = ctx.enter_context(nc.sbuf_tensor("x1", [P, TILES, D], F32))
        x = ctx.enter_context(nc.sbuf_tensor("x", [P, TILES, D], F32))
        x_loaded, added, stored = (ctx.enter_context(nc.semaphore(n)) for n in ("x_loaded", "x_added", "out_stored"))
        scratch = {n: nc.dram_tensor("scratch_" + n, [P, c], F32).ap()
                   for n, c in (("qv", TILES * P + 1), ("qu", TILES * P), ("k", TILES * P), ("bp", SEQ))}
        tiled = "(t p) d -> p t d"
        with nc.Block() as block:
            @block.sync
            def _(sp):
                sp.dma_start(x1[:, :, :], x_in.rearrange("b s d -> (b s) d").rearrange(tiled, p=P)).then_inc(x_loaded, 16)
                sp.wait_ge(x_loaded, 16)
        relative_attention(nc, x1, attention, scratch)
        layer_norm_tiles(nc, x1, x, "norm2")
        local_layers(nc, x, layers)
        with nc.Block() as block:
            @block.vector
            def _(dve):
                nc.vector.tensor_tensor(x[:, :, :], x[:, :, :], x1[:, :, :], ALU.add).then_inc(added, 1)

            @block.sync
            def _(sp):
                sp.wait_ge(added, 1)
                sp.dma_start(out.rearrange("b s d -> (b s) d").rearrange(tiled, p=P), x[:, :, :]).then_inc(stored, 16)
                sp.wait_ge(stored, 16)


def attention_layout(a):
    import numpy as np

    freq = 1.0 / 10000.0 ** (2.0 * np.arange(D // 2, dtype=np.float64) / D)
    turn = -(1.0 + np.arange(SEQ, dtype=np.float64))[None, :] * freq[:, None]
    col = np.arange(SEQ + 1, dtype=np.float64)[None, :]
    fcols = [np.concatenate([np.sin((col + off) * freq[:, None]), np.cos((col + off) * freq[:, None])]) for off in (SEQ, 0)]
    i, j = np.arange(P)[:, None], np.arange(P + 1)[None, :]
    wp = a["Wp"].reshape(D, H0, DP).transpose(1, 2, 0)
    cols = np.zeros((P, 8), np.float32)
    for n, c in enumerate((a["bq"], a["bk"], a["u"].reshape(-1), a["v"].reshape(-1), a["bp"])):
        cols[:, n] = c
    return {
        "turns": np.stack([np.concatenate([np.cos(turn)] * 2), np.concatenate([-np.sin(turn), np.sin(turn)])], 1
                          ).astype(np.float32),
        "fcols": np.stack(fcols, 1).astype(np.float32),
        "mask": np.concatenate([j <= i, j >= i + 2], 1).astype(np.float32),
        "ident": np.eye(P, dtype=np.float32),
        "wproj": np.stack([a[n] for n in ("Wq", "Wk", "Wv", "Wo")], 1),
        "cols": cols,
        "rows": np.broadcast_to(np.stack([a["bv"], a["bo"]])[None], (P, 2, D)),
        "wpT": np.stack([wp, np.concatenate([wp[:, :, D // 2:], wp[:, :, :D // 2]], 2)], 2),
    }


def layers_layout(f):
    import numpy as np

    w1 = np.zeros((DEPTH, D, 2, FCH * FW), np.float32)
    w1[:, :, :, :DFF] = f["W1"].reshape(DEPTH, D, 2, DFF)
    b1 = np.zeros((DEPTH, 2, FCH * FW), np.float32)
    b1[:, :, :DFF] = f["b1"].reshape(DEPTH, 2, DFF)
    w2 = np.zeros((DEPTH, FCH * FW, D), np.float32)
    w2[:, :DFF] = f["W2"]
    half = np.arange(0, DH, 2, dtype=np.float64)
    t = np.arange(SEQ, dtype=np.float64)
    freqs = np.concatenate([t[:, None] * (1.0 / 10000.0 ** (half / DH))[None, :]] * 2, -1)
    base = (half + 0.4 * DH) / (1.4 * DH)
    scale = np.concatenate([base[None, :] ** ((t - SEQ // 2) / (W // 2))[:, None]] * 2, -1)
    sign = np.where(np.arange(DH) < DH // 2, 1.0, -1.0)
    rope = np.empty((P, 2, SEQT * 2, DH), np.float32)
    for n, sc in enumerate((scale, 1.0 / scale)):
        for part, table in enumerate((np.cos(freqs) * sc, np.sin(freqs) * sc * sign)):
            rope[:, n, part::2, :] = table.reshape(SEQT, P, DH).transpose(1, 0, 2)
    return {
        "wqkv": f["Wqkv"],
        "wo": f["Wo"].reshape(DEPTH, PAIRS, P, D).transpose(0, 2, 1, 3),
        "w1": w1.reshape(DEPTH, D, 2 * FCH * FW),
        "w2": w2.reshape(DEPTH, FCH, FW, D).transpose(0, 2, 1, 3),
        "b1": b1.reshape(DEPTH, 2 * FCH, FW).transpose(0, 2, 1),
        "ln": np.stack([f["ln_g"], f["ln_b"]], -1),
        "b2": np.broadcast_to(f["b2"][:, None, :], (DEPTH, P, D)),
        "qk": np.broadcast_to(np.stack([f["q_scale"], f["k_scale"]], 1)[:, None], (DEPTH, P, 2, DH)),
        "rope": rope,
        "ident": np.eye(P, dtype=np.float32),
    }


def kernel(**inputs):
    import numpy as np
    import concourse.bacc as bacc
    from concourse.bass_utils import run_bass_kernel_spmd

    parts = {}
    for group, prefix, layout in (("a", "L0_attn_", attention_layout), ("l", "L0_ffn_", layers_layout)):
        parts[group] = layout({n[len(prefix):]: np.asarray(a) for n, a in inputs.items()
                               if n.startswith(prefix) and n != "L0_attn_x"})
    nc = bacc.Bacc("TRN2", target_bir_lowering=False, num_devices=1)
    arrays, aps = {}, {}

    def declare(name, a):
        arrays[name] = np.ascontiguousarray(a)
        return nc.dram_tensor(name, arrays[name].shape, mybir.dt.from_np(arrays[name].dtype), kind="ExternalInput").ap()

    x_in = declare("in_x", np.asarray(inputs["L0_attn_x"]))
    for group, named in parts.items():
        aps[group] = {n: declare(f"in_{group}_{n}", a) for n, a in named.items()}
    out = nc.dram_tensor("out_0_dram", (BATCH, SEQ, D), F32, kind="ExternalOutput").ap()
    whole_kernel(nc, x_in, out, aps["a"], aps["l"])
    r = run_bass_kernel_spmd(nc, [arrays], core_ids=[0])
    return r.results[0]["out_0_dram"]
```

```python
from contextlib import ExitStack

import concourse.bass as bass
from concourse import mybir

F32, BF16 = mybir.dt.float32, mybir.dt.bfloat16
ALU, ACT, AX = mybir.AluOpType, mybir.ActivationFunctionType, mybir.AxisListType

P = 128
D = 128
BATCH, SEQ = 4, 512
SEQT = SEQ // P
TILES = BATCH * SEQT
EPS = 1e-5

H0, DP = 16, 8
SCALE0 = DP ** -0.5

DEPTH, HEADS, DH, W = 6, 16, 64, 32
INNER = HEADS * DH
PAIRS = HEADS // 2
W2 = 2 * W
WT = P // W
DFF = int(D * 4 * 2 / 3)
FCH = 3
FW = -(-DFF // FCH)
QK_SCALE = 8.0
NORM_FLOOR = 1e-24
MASKED = -1e30


class Tally:

    def __init__(self, sem):
        self.sem, self.base, self.n = sem, 0, 0

    def add(self, ins):
        ins.then_inc(self.sem, 1)
        self.n += 1

    def settle(self, eng):
        eng.wait_ge(self.sem, self.base + self.n)

    def close(self):
        self.base, self.n = self.base + self.n, 0


def at_least(eng, sem, count):
    if not isinstance(count, int) or count > 0:
        eng.wait_ge(sem, count)


def stand(eng, sem):
    eng.sem_inc(sem, 1)


def rounds(eng, head, tail, body, own=None, each=0):
    for g in head:
        body(g)
    if own is not None:
        own.close()
        before = own.base
    with eng.Fori(head[-1] + 1, tail[0]) as g:
        if own is not None:
            own.base = eng.snap(before + (g - head[-1] - 1) * each)
        body(g)
    if own is not None:
        assert own.n == each, (own.n, each)
        own.base, own.n = before + (tail[0] - head[-1] - 1) * each, 0
    for g in tail:
        body(g)


def local_layers(nc, x, w):
    with ExitStack() as ctx:
        def sb(name, shape, dt=F32):
            return ctx.enter_context(nc.sbuf_tensor(name, shape, dt))

        wqkv = sb("wqkv", [P, 2, 3 * INNER])
        wo = sb("wo", [P, 2, PAIRS, D])
        w1ring = sb("w1ring", [P, 2, 2 * FCH * FW])
        w2 = sb("w2", [FW, 2, FCH, D])
        b1 = sb("b1", [FW, 2, 2 * FCH])
        ln = sb("ln", [P, 2, 2])
        b2 = sb("b2", [P, 2, D])
        qkscale = sb("qkscale", [P, 2, 2, DH])
        w1 = sb("w1", [P, 2 * FCH * FW])
        rope = sb("rope", [P, 2, SEQT * 2, DH])
        ropes = sb("ropes", [P, 2, 2, SEQT * 2, DH])
        ident = sb("ident_l", [P, P])
        identb = sb("identb", [P, P], BF16)
        bias = sb("bias", [P, 2, 8, W2], BF16)

        xs = sb("xs", [P, SEQT, D])
        xsf = sb("xsf", [P, SEQT, D])
        xT = sb("xT", [P, 2, P])
        squares = sb("squares", [P, 2, INNER])
        turned = sb("turned", [P, 2, 2, INNER])
        roped = sb("roped", [P, 2, INNER])
        ss = sb("ss", [P, 2 * HEADS])
        rnorm = sb("rnorm", [P, 2, HEADS])
        power = sb("power", [P, HEADS])
        eps = sb("eps", [P, SEQT])
        qT = sb("qT", [P, PAIRS, WT, 2, W])
        kT = sb("kT", [P, 2, PAIRS, W + P])
        v = sb("v", [P, 2, 2, PAIRS, DH])
        vwin = sb("vwin", [P, 2 * WT, PAIRS, P])
        probs = sb("probs", [P, 2, HEADS, W2])
        smax = sb("smax", [P, HEADS])
        rsum = sb("rsum", [P, 2, HEADS])
        pT = sb("pT", [P, PAIRS, P])
        attended = sb("attended", [P, PAIRS, P])
        oT = sb("oT", [P, PAIRS, P])
        stats = sb("stats", [P, SEQT, 6])
        meanvar = sb("meanvar", [P, SEQT, 2])
        rstd = sb("rstd", [P, SEQT])
        xn = sb("xn", [P, SEQT, D])
        xnT = sb("xnT", [P, SEQ])
        gelu = sb("gelu", [FW, 2, SEQ])
        hT = sb("hT", [FW, FCH, SEQ])

        ring = ctx.enter_context(nc.psum_tensor("ring", [P, 3, 1024], F32))
        tpose = ctx.enter_context(nc.psum_tensor("tpose", [P, 512], F32))
        yps = ctx.enter_context(nc.psum_tensor("yps", [P, 512], F32))

        names = ("cleared loaded ready weights xs_in xsf_in v_even v_odd v_tail x_turned xT_copied "
                 "p_turned p_copied q_turned qT_copied k_turned kT_copied o_summed o_copied o_turned oT_copied scored "
                 "scores_taken exped y_made y_added q_made q_squared q_rotated k_made k_squared k_rotated v_made "
                 "v_copied squares_summed var_made rstd_made qk_roped probs_ready ropes_made w1_copied xn_made xn_turned "
                 "xnT_copied h_made gelu_made h_ready f_made x_done stood dve_own pool_own act_own").split()
        s = {n: ctx.enter_context(nc.semaphore("l_" + n)) for n in names}
        GROUPS = DEPTH * BATCH
        HEAD, TAIL = (0, 1), (GROUPS - 1, GROUPS, GROUPS + 1)
        VTAIL = 2 * 16
        VPLACED = 4 * WT * 16 - VTAIL
        CLEARED = 6
        LOADS = 8 * 16
        XSHIFT = 3 * 16

        STEP = ("Q", "OT", "K", "V", "QT", "KT", "PT", "S", "O")
        LAG = {"PT": 2, "QT": 1, "KT": 1, "OT": 3, "O": 2, "S": 1, "Q": 0, "K": 0, "V": 0}
        USES = [(kind, step) for step in range(SEQT) for kind in STEP] + [("H", c) for c in range(FCH)]
        FREED = {"PT": ("p_copied",), "QT": ("qT_copied",), "KT": ("kT_copied",), "OT": ("oT_copied",), "O": ("o_copied",),
                 "S": ("scores_taken",), "Q": ("q_rotated",), "K": ("k_rotated",), "V": ("v_copied",),
                 "H": ("gelu_made", "h_ready")}
        assert len(USES) % 3 == 0

        def count(kind, step, g):
            if kind == "H":
                n, last = FCH * (g - 1) + step + 1, FCH * GROUPS
            else:
                n, last = SEQT * g + step - LAG[kind] + 1, SEQT * GROUPS
            return None if isinstance(g, int) and not 0 < n <= last else n

        def slot(kind, step):
            return USES.index((kind, step)) % 3

        def take(pe, kind, step, g):
            u = USES.index((kind, step)) - 3
            while not isinstance(g, int) or g + u // len(USES) >= 0:
                held = USES[u % len(USES)]
                before = count(*held, g + u // len(USES))
                if before is not None:
                    for name in FREED[held[0]]:
                        pe.wait_ge(s[name], before * (2 if held[0] in ("S", "QT") else 1))
                    break
                u -= 3
            return ring[:, slot(kind, step), :]

        def live(t):
            return not isinstance(t, int) or 0 <= t < SEQT * GROUPS

        def layer_of(g):
            return (g // BATCH) % 2

        def weights_in(eng, g):
            eng.wait_ge(s["weights"], LOADS * (g // BATCH + 1))

        block = ctx.enter_context(nc.Block())

        @block.sync
        def _(sp):
            def load_layer(layer, parity):
                stand(sp, s["stood"])
                for dst, src in ((wqkv[:, parity, :], w["wqkv"]), (wo[:, parity, :, :], w["wo"]),
                                 (w1ring[:, parity, :], w["w1"]), (w2[:, parity, :, :], w["w2"]),
                                 (b1[:, parity, :], w["b1"]), (ln[:, parity, :], w["ln"]),
                                 (b2[:, parity, :], w["b2"]), (qkscale[:, parity, :, :], w["qk"])):
                    sp.dma_start(dst, src[layer]).then_inc(s["weights"], 16)

            def shift_in(dst, g, signal):
                stand(sp, s["stood"])
                tiles = x[:, bass.ds(g % BATCH * SEQT, SEQT), :]
                before = x[:, bass.ds(g % BATCH * SEQT, SEQT - 1), :]
                sp.dma_start(dst[:, :, 0:D // 2], tiles[:, :, 0:D // 2]).then_inc(signal, 16)
                sp.dma_start(dst[1:P, :, D // 2:D], tiles[0:P - 1, :, D // 2:D]).then_inc(signal, 16)
                sp.dma_start(dst[0:1, 1:SEQT, D // 2:D], before[P - 1:P, :, D // 2:D]).then_inc(signal, 16)

            def body(g):
                for step in range(SEQT):
                    t = SEQT * g + step
                    if step == 2 and live(SEQT * (g - 1)):
                        sp.wait_ge(s["y_added"], SEQT * g)
                        stand(sp, s["stood"])
                        at_least(sp, s["xn_made"], g - 1)
                        shift_in(xsf, g - 1, s["xsf_in"])
                    if step == 2 and live(SEQT * (g + 1)):
                        at_least(sp, s["x_done"], g + 1 - BATCH + 1)
                        stand(sp, s["stood"])
                        sp.wait_ge(s["x_turned"], SEQT * (g + 1))
                        shift_in(xs, g + 1, s["xs_in"])
                    if live(t):
                        placed = s["v_odd" if step % 2 else "v_even"]
                        sp.wait_ge(s["v_copied"], t + 1)
                        stand(sp, s["stood"])
                        at_least(sp, s["o_summed"], t - 1)
                        for win in range(WT):
                            for r in range(2):
                                at, of = (step % 2) * WT + win, slice(r * DH, r * DH + DH)
                                now = v[W * win:W * win + W, step % 2, r, :, :]
                                before = v[W * win - W:W * win, step % 2, r, :, :] if win else v[P - W:P, 1 - step % 2, r, :, :]
                                sp.dma_start(vwin[W2 * r:W2 * r + W, at, :, of], before
                                             ).then_inc(placed if win else s["v_tail"], 16)
                                if win == 0:
                                    continue
                                sp.dma_start(vwin[W2 * r + W:W2 * r + W2, at, :, of], now).then_inc(placed, 16)
                        for r in range(2):
                            sp.dma_start(vwin[W2 * r + W:W2 * r + W2, (step % 2) * WT, :, r * DH:r * DH + DH],
                                         v[0:W, step % 2, r, :, :]).then_inc(placed, 16)

            for dst, src in ((rope[:, :, :, :], w["rope"]), (ident[:, :], w["ident"])):
                sp.dma_start(dst, src).then_inc(s["loaded"], 16)
            sp.wait_ge(s["cleared"], CLEARED)
            shift_in(xs, 0, s["xs_in"])
            load_layer(0, 0)

            def layer_groups(layer, next_parity):
                for b in range(BATCH):
                    body(BATCH * layer + b)
                    if b == 1 and next_parity is not None:
                        at_least(sp, s["x_done"], BATCH * layer)
                        sp.wait_ge(s["weights"], LOADS * (layer + 1))
                        load_layer(layer + 1, next_parity)

            layer_groups(0, 1)

            with sp.Fori(0, (DEPTH - 2) // 2) as two:
                layer_groups(2 * two + 1, 0)
                layer_groups(2 * two + 2, 1)
            layer_groups(DEPTH - 1, None)
            body(GROUPS)

        @block.gpsimd
        def _(pool):
            own = Tally(s["pool_own"])
            nc.gpsimd.memset(v[:, 1, :, :, :], 0.0).then_inc(s["cleared"], 1)
            nc.gpsimd.memset(kT[:, 1, :, P:P + W], 0.0).then_inc(s["cleared"], 1)
            nc.gpsimd.memset(xs[0:1, :, :], 0.0).then_inc(s["cleared"], 1)
            nc.gpsimd.memset(xsf[0:1, :, :], 0.0).then_inc(s["cleared"], 1)
            nc.gpsimd.memset(vwin[:, :, :, :], 0.0).then_inc(s["cleared"], 1)
            nc.gpsimd.memset(qT[:, :, :, :, :], 0.0).then_inc(s["cleared"], 1)
            own.add(nc.gpsimd.memset(power[:, :], -0.5))
            own.add(nc.gpsimd.memset(eps[:, :], EPS))
            own.add(nc.gpsimd.memset(bias[:, :, :, :], 0.0))
            own.settle(pool)
            for first in range(2):
                for win in range(WT):
                    view = bias[W * win:W * win + W, first, :, :]
                    own.add(nc.gpsimd.affine_select(out=view, in_=view, compare_op=ALU.is_ge, fill=MASKED, base=0,
                                                    pattern=[[0, 8], [1, W2]], channel_multiplier=-1))
                    own.settle(pool)
                    own.add(nc.gpsimd.affine_select(out=view, in_=view, compare_op=ALU.is_ge, fill=MASKED, base=W,
                                                    pattern=[[0, 8], [-1, W2]], channel_multiplier=1))
                    own.settle(pool)
            own.add(nc.gpsimd.memset(bias[0:2 * W, 1, :, 0:W], MASKED))
            own.settle(pool)
            pool.wait_ge(s["loaded"], 32)
            nc.gpsimd.tensor_copy(identb[:, :], ident[:, :]).then_inc(s["ready"], 1)
            own.close()

            def body(g):
                if live(SEQT * g):
                    weights_in(pool, g)
                    at_least(pool, s["k_rotated"], SEQT * (g - 1))
                    scales = qkscale[:, layer_of(g), :, :]
                    for n in range(2):
                        scale = scales[:, n:n + 1, :].broadcast_to([P, SEQT * 2, DH])
                        nc.gpsimd.tensor_tensor(ropes[:, g % 2, n, :, :], rope[:, n, :, :], scale,
                                                ALU.mult).then_inc(s["ropes_made"], 1)
                for step in range(SEQT):
                    t = SEQT * g + step
                    if live(t):
                        for n, name in enumerate("qk"):
                            pool.wait_ge(s[name + "_rotated"], t + 1)
                            at_least(pool, s[name + "_turned"], t)
                            halves = [y.rearrange("p (h s e) -> p h s e", s=2, e=DH // 2)
                                      for y in (turned[:, n, 0, :], turned[:, n, 1, :], roped[:, n, :])]
                            for side in range(2):
                                own.add(nc.gpsimd.tensor_tensor(halves[2][:, :, side, :], halves[0][:, :, side, :],
                                                                halves[1][:, :, 1 - side, :], ALU.add))
                            pool.wait_ge(s["squares_summed"], 2 * t + n + 1)
                            sums = ss[:, n * HEADS:(n + 1) * HEADS]
                            at_least(pool, s["qk_roped"], 2 * t + n - 1)
                            own.add(nc.gpsimd.tensor_tensor(rnorm[:, n, :], sums, power[:, :], ALU.pow))
                            own.settle(pool)
                            norm = rnorm[:, n, :].unsqueeze(2).broadcast_to([P, HEADS, DH])
                            whole = roped[:, n, :].rearrange("p (h d) -> p h d", d=DH)
                            nc.gpsimd.tensor_tensor(whole, whole, norm, ALU.mult).then_inc(s["qk_roped"], 1)
                    if step == 2 and live(SEQT * (g - 1)):
                        pool.wait_ge(s["var_made"], g)
                        own.add(nc.gpsimd.tensor_tensor(rstd[:, :], meanvar[:, :, 1], eps[:, :], ALU.add))
                        own.settle(pool)
                        nc.gpsimd.tensor_tensor(rstd[:, :], rstd[:, :], power[:, 0:SEQT], ALU.pow
                                                ).then_inc(s["rstd_made"], 1)
                        at_least(pool, s["h_made"], FCH * (g - 1))
                        nc.gpsimd.tensor_copy(w1[:, :], w1ring[:, layer_of(g - 1), :]
                                              ).then_inc(s["w1_copied"], 1)

            rounds(pool, HEAD, TAIL, body, own, 6 * SEQT + 1)

        @block.scalar
        def _(act):
            own = Tally(s["act_own"])

            def square(a, n, step):
                name = "qk"[n]
                act.wait_ge(s[name + "_made"], a + 1)
                at_least(act, s["squares_summed"], 2 * a - 1 + n)
                nc.scalar.activation(squares[:, n, :], ring[:, slot(name.upper(), step), :],
                                     ACT.Square).then_inc(s[name + "_squared"], 1)

            def copy_x(t, parity):
                act.wait_ge(s["x_turned"], t + 1)
                at_least(act, s["v_made"], t - 1)
                nc.scalar.copy(xT[:, parity, :], tpose[:, 0:P]).then_inc(s["xT_copied"], 1)

            def body(g):
                if live(SEQT * g):
                    weights_in(act, g)
                for step in range(SEQT):
                    a, b, c, d = (SEQT * g + step - lag for lag in range(4))
                    pa, pb = step % 2, (step + 1) % 2
                    if live(a):
                        square(a, 0, step)
                    if live(d):
                        act.wait_ge(s["o_turned"], d + 1)
                        at_least(act, s["y_made"], d)
                        nc.scalar.copy(oT[:, :, :].rearrange("p a b -> p (a b)"),
                                       ring[:, slot("OT", step), :]).then_inc(s["oT_copied"], 1)
                    if live(a):
                        square(a, 1, step)
                        act.wait_ge(s["v_made"], a + 1)
                        at_least(act, s["v_odd" if pa else "v_even"], (2 * g + step // 2) * VPLACED)
                        at_least(act, s["v_tail"], a * VTAIL)
                        nc.scalar.copy(v[:, pa, :, :, :].rearrange("p r (a b) e -> p r a (b e)", b=2),
                                       ring[:, slot("V", step), :].rearrange("p (a r x) -> p r a x", r=2, x=2 * DH)
                                       ).then_inc(s["v_copied"], 1)
                    if live(a + 1):
                        copy_x(a + 1, pb)
                    if live(b):
                        act.wait_ge(s["q_turned"], b + 1)
                        at_least(act, s["scored"], 2 * b)
                        if isinstance(b, int) and b == 0:
                            act.wait_ge(s["cleared"], CLEARED)
                        nc.scalar.copy(qT[0:DH, :, :, 0, :].rearrange("p a w i -> p (a w) i"),
                                       ring[0:DH, slot("QT", step), :].rearrange("p (a i) -> p a i", i=W)
                                       ).then_inc(s["qT_copied"], 1)
                        at_least(act, s["kT_copied"], b)
                        own.add(nc.scalar.copy(kT[:, pb, :, 0:W], kT[:, 1 - pb, :, P:P + W]))
                        act.wait_ge(s["k_turned"], b + 1)
                        own.settle(act)
                        nc.scalar.copy(kT[:, pb, :, W:W + P],
                                       ring[:, slot("KT", step), :].rearrange("p (a b) -> p a b", b=P)
                                       ).then_inc(s["kT_copied"], 1)
                    if live(c):
                        act.wait_ge(s["p_turned"], c + 1)
                        at_least(act, s["o_summed"], c)
                        nc.scalar.copy(pT[:, :, :].rearrange("p a b -> p (a b)"),
                                       ring[:, slot("PT", step), :]).then_inc(s["p_copied"], 1)
                    if step == 3 and live(SEQT * (g - 1)):
                        act.wait_ge(s["xn_turned"], g)
                        at_least(act, s["h_made"], FCH * (g - 1))
                        of = ln[:, layer_of(g - 1), :]
                        nc.scalar.activation(xnT[:, :], tpose[:, :], ACT.Identity,
                                             scale=of[:, 0:1], bias=of[:, 1:2]).then_inc(s["xnT_copied"], 1)
                    if live(b):
                        for half in range(2):
                            act.wait_ge(s["scores_taken"], 2 * b + half + 1)
                            flat = probs[:, pb, half * PAIRS:(half + 1) * PAIRS, :].rearrange("p h k -> p (h k)")
                            nc.scalar.activation(flat, flat, ACT.Exp, scale=QK_SCALE).then_inc(s["exped"], 1)
                    if live(c):
                        act.wait_ge(s["o_summed"], c + 1)
                        at_least(act, s["o_turned"], c)
                        nc.scalar.copy(attended[:, :, :].rearrange("p a b -> p (a b)"),
                                       ring[:, slot("O", step), :]).then_inc(s["o_copied"], 1)
                if live(SEQT * (g - 1)):
                    of = b1[:, layer_of(g - 1), :]
                    for c in range(FCH):
                        n = FCH * (g - 1) + c
                        act.wait_ge(s["h_made"], n + 1)
                        at_least(act, s["h_ready"], FCH * (g - 1) if c < 2 else n - 1)
                        nc.scalar.activation(gelu[:, c % 2, :], ring[0:FW, slot("H", c), 0:SEQ], ACT.Gelu,
                                             bias=of[:, FCH + c:FCH + c + 1]).then_inc(s["gelu_made"], 1)

            copy_x(0, 0)
            rounds(act, HEAD, TAIL, body, own, SEQT)

        @block.tensor
        def _(pe):
            def project(kind, step, g):
                out = take(pe, kind, step, g)
                for half in range(2):
                    last = nc.tensor.matmul(
                        out[:, half * 512:(half + 1) * 512], xT[:, step % 2, :],
                        wqkv[:, layer_of(g), bass.ds("QKV".index(kind) * INNER + half * 512, 512)],
                        start=True, stop=True)
                last.then_inc(s[kind.lower() + "_made"], 1)

            def turn_pairs(b, n, kind, signal, step, g):
                pe.wait_ge(s["qk_roped"], 2 * b + n + 1)
                out = take(pe, kind, step, g)
                for pair in range(PAIRS):
                    last = nc.tensor.transpose(out[:, pair * P:(pair + 1) * P],
                                               roped[:, n, pair * P:(pair + 1) * P], ident[:, :])
                last.then_inc(s[signal], 1)

            def turn_x(t, step):
                at_least(pe, s["xT_copied"], t)
                nc.tensor.transpose(tpose[:, 0:P], xs[:, step, :], ident[:, :]).then_inc(s["x_turned"], 1)

            def body(g):
                if live(SEQT * g):
                    weights_in(pe, g)
                for step in range(SEQT):
                    a, b, c, d = (SEQT * g + step - lag for lag in range(4))
                    pa, pb = step % 2, (step + 1) % 2
                    if live(a):
                        pe.wait_ge(s["xT_copied"], a + 1)
                        project("Q", step, g)
                    if live(d):
                        pe.wait_ge(s["o_copied"], d + 1)
                        out = take(pe, "OT", step, g)
                        for pair in range(PAIRS):
                            last = nc.tensor.transpose(out[:, pair * P:(pair + 1) * P], attended[:, pair, :], ident[:, :])
                        last.then_inc(s["o_turned"], 1)
                    if live(a):
                        project("K", step, g)
                        project("V", step, g)
                    if live(a + 1):
                        if step == 3:
                            pe.wait_ge(s["xs_in"], XSHIFT * (g + 2))
                        if step == 0:
                            at_least(pe, s["xnT_copied"], g - 1)
                        turn_x(a + 1, (step + 1) % SEQT)
                    if live(d):
                        pe.wait_ge(s["oT_copied"], d + 1)
                        at_least(pe, s["y_added"], d)
                        if step:
                            at_least(pe, s["x_done"], g - 1)
                        for pair in range(PAIRS):
                            last = nc.tensor.matmul(yps[:, 0:D], oT[:, pair, :], wo[:, layer_of(d // SEQT), pair, :],
                                                    start=pair == 0, stop=pair == PAIRS - 1)
                        last.then_inc(s["y_made"], 1)
                    if live(b):
                        turn_pairs(b, 0, "QT", "q_turned", step, g)
                    if live(b):
                        turn_pairs(b, 1, "KT", "k_turned", step, g)
                    if live(c):
                        pe.wait_ge(s["probs_ready"], c + 1)
                        out = take(pe, "PT", step, g)
                        for pair in range(PAIRS):
                            last = nc.tensor.transpose(
                                out[:, pair * P:(pair + 1) * P],
                                probs[:, pa, 2 * pair:2 * pair + 2, :].rearrange("p h k -> p (h k)"), ident[:, :])
                        last.then_inc(s["p_turned"], 1)
                    if step == 0 and live(SEQT * (g - 2)):
                        pe.wait_ge(s["h_ready"], FCH * (g - 1))
                        pe.wait_ge(s["y_added"], min(SEQT * g - 2, SEQT * GROUPS) if isinstance(g, int) else SEQT * g - 2)
                        for tile in range(SEQT):
                            for chunk in range(FCH):
                                last = nc.tensor.matmul(yps[:, tile * D:(tile + 1) * D],
                                                        hT[:, chunk, tile * P:(tile + 1) * P],
                                                        w2[:, layer_of(g - 2), chunk, :],
                                                        start=chunk == 0, stop=chunk == FCH - 1)
                        last.then_inc(s["f_made"], 1)
                    if step == 3 and live(SEQT * (g - 1)):
                        pe.wait_ge(s["xn_made"], g)
                        pe.wait_ge(s["xT_copied"], min(a + 2, SEQT * GROUPS) if isinstance(a, int) else a + 2)
                        for tile in range(SEQT):
                            last = nc.tensor.transpose(tpose[:, tile * P:(tile + 1) * P], xn[:, tile, :], ident[:, :])
                        last.then_inc(s["xn_turned"], 1)
                    if live(b):
                        pe.wait_ge(s["qT_copied"], 2 * (b + 1))
                        pe.wait_ge(s["kT_copied"], b + 1)
                        out = take(pe, "S", step, g)
                        for half in range(2):
                            nc.tensor.matmul(out[:, half * 512:(half + 1) * 512], identb[:, :],
                                             bias[:, 1 if step == 1 and half == 0 else 0, :, :].rearrange("p h k -> p (h k)"),
                                             start=True, stop=False, skip_group_check=True)
                        for win in range(WT):
                            rows = slice((win % 2) * W2, (win % 2) * W2 + W2)
                            for pair in range(PAIRS):
                                at = (win // 2) * 512 + pair * W2
                                last = nc.tensor.matmul(
                                    out[rows, at:at + W2], qT[:, pair, win, :, :].rearrange("p h i -> p (h i)"),
                                    kT[:, pb, pair, W * win:W * win + W2],
                                    start=False, stop=True, skip_group_check=True)
                            if win % 2:
                                last.then_inc(s["scored"], 1)
                    if live(c):
                        pe.wait_ge(s["p_copied"], c + 1)
                        even = step % 2 == 0
                        pe.wait_ge(s["v_even" if even else "v_odd"], (2 * g + (step - 2) // 2 + 1) * VPLACED)
                        pe.wait_ge(s["v_tail"], (c + 1) * VTAIL)
                        out = take(pe, "O", step, g)
                        stand(pe, s["stood"])
                        for win in range(WT):
                            for pair in range(PAIRS):
                                columns = ((win % 2) * 2 + pair % 2) * W
                                last = nc.tensor.matmul(
                                    out[W * win:W * win + W, pair * P:(pair + 1) * P],
                                    pT[:, (win // 2) * (PAIRS // 2) + pair // 2, columns:columns + W],
                                    vwin[:, pa * WT + win, pair, :], start=True, stop=True)
                        last.then_inc(s["o_summed"], 1)
                if live(SEQT * (g - 1)):
                    pe.wait_ge(s["xnT_copied"], g)
                    pe.wait_ge(s["w1_copied"], g)
                    for c in range(FCH):
                        out = take(pe, "H", c, g)
                        for n, part in enumerate((FCH + c, c)):
                            last = nc.tensor.matmul(out[0:FW, n * 512:(n + 1) * 512], w1[:, part * FW:(part + 1) * FW],
                                                    xnT[:, :], start=True, stop=True)
                        last.then_inc(s["h_made"], 1)

            pe.wait_ge(s["loaded"], 32)
            pe.wait_ge(s["ready"], 1)
            pe.wait_ge(s["cleared"], CLEARED)
            pe.wait_ge(s["xs_in"], XSHIFT)
            turn_x(0, 0)
            rounds(pe, HEAD, TAIL, body)

        @block.vector
        def _(dve):
            own = Tally(s["dve_own"])

            def body(g):
                if live(SEQT * g):
                    weights_in(dve, g)
                    dve.wait_ge(s["ropes_made"], 2 * (g + 1))
                for step in range(SEQT):
                    a, b, c, d = (SEQT * g + step - lag for lag in range(4))
                    pa, pb = step % 2, (step + 1) % 2
                    if live(a):
                        for n, name in enumerate("qk"):
                            dve.wait_ge(s[name + "_squared"], a + 1)
                            at_least(dve, s["qk_roped"], 2 * a - 1 + n)
                            heads = ring[:, slot(name.upper(), step), :].rearrange("p (h d) -> p h d", d=DH)
                            for part in range(2):
                                table = ropes[:, g % 2, n, 2 * step + part:2 * step + part + 1, :].broadcast_to([P, HEADS, DH])
                                ins = nc.vector.tensor_tensor(
                                    turned[:, n, part, :].rearrange("p (h d) -> p h d", d=DH), heads, table, ALU.mult)
                            ins.then_inc(s[name + "_rotated"], 1)
                        for n in range(2):
                            sums = ss[:, n * HEADS:(n + 1) * HEADS]
                            own.add(nc.vector.tensor_reduce(sums, squares[:, n, :].rearrange("p (h d) -> p h d", d=DH),
                                                            AX.X, ALU.add))
                            own.settle(dve)
                            nc.vector.tensor_scalar(sums, sums, NORM_FLOOR, None, ALU.max
                                                    ).then_inc(s["squares_summed"], 1)
                    if step == 3 and live(SEQT * (g - 1)):
                        at_least(dve, s["xn_turned"], g - 1)
                        dve.wait_ge(s["rstd_made"], g)
                        for tile in range(SEQT):
                            ins = nc.vector.tensor_scalar(xn[:, tile, :], xsf[:, tile, :], meanvar[:, tile, 0:1],
                                                          rstd[:, tile:tile + 1], ALU.subtract, ALU.mult)
                        ins.then_inc(s["xn_made"], 1)
                    if live(d):
                        dve.wait_ge(s["y_made"], d + 1)
                        row = x[:, d % TILES, :]
                        nc.vector.tensor_tensor(row, yps[:, 0:D], row, ALU.add).then_inc(s["y_added"], 1)
                    if live(b):
                        dve.wait_ge(s["q_turned"], b + 1)
                        at_least(dve, s["scored"], 2 * b)
                        if isinstance(b, int) and b == 0:
                            dve.wait_ge(s["cleared"], CLEARED)
                        nc.vector.tensor_copy(qT[DH:P, :, :, 1, :].rearrange("p a w i -> p (a w) i"),
                                              ring[DH:P, slot("QT", step), :].rearrange("p (a i) -> p a i", i=W)
                                              ).then_inc(s["qT_copied"], 1)
                    if step == 0 and live(SEQT * (g - 2)):
                        tiles = x[:, bass.ds((g - 2) % BATCH * SEQT, SEQT), :]
                        dve.wait_ge(s["f_made"], g - 1)
                        nc.vector.tensor_tensor(tiles, yps[:, :].rearrange("p (t d) -> p t d", d=D), tiles,
                                                ALU.add).then_inc(s["x_done"], 1)
                    if step == 2 and live(SEQT * (g - 1)):
                        dve.wait_ge(s["xsf_in"], XSHIFT * g)
                        for tile in range(SEQT):
                            own.add(nc.vector.bn_stats(stats[:, tile, :], xsf[:, tile, :]))
                        own.settle(dve)
                        tiles = x[:, bass.ds((g - 1) % BATCH * SEQT, SEQT), :]
                        lp = layer_of(g - 1)
                        own.add(nc.vector.tensor_tensor(tiles, tiles,
                                                        b2[:, lp, :].unsqueeze(1).broadcast_to([P, SEQT, D]), ALU.add))
                        for tile in range(SEQT):
                            ins = nc.vector.bn_aggr(meanvar[:, tile, :], stats[:, tile, :])
                        ins.then_inc(s["var_made"], 1)
                    if live(b):
                        halves = [(ring[:, slot("S", step), half * 512:(half + 1) * 512].rearrange("p (h k) -> p h k", k=W2),
                                   probs[:, pb, half * PAIRS:(half + 1) * PAIRS, :],
                                   slice(half * PAIRS, (half + 1) * PAIRS)) for half in range(2)]
                        for half, (scores, _, heads) in enumerate(halves):
                            dve.wait_ge(s["scored"], 2 * b + half + 1)
                            own.add(nc.vector.tensor_reduce(smax[:, heads], scores, AX.X, ALU.max))
                        at_least(dve, s["p_turned"], b - 1)
                        own.settle(dve)
                        for scores, less, heads in halves:
                            nc.vector.tensor_tensor(less, scores, smax[:, heads].unsqueeze(2).broadcast_to([P, PAIRS, W2]),
                                                    ALU.subtract).then_inc(s["scores_taken"], 1)
                        for half, (_, exps, heads) in enumerate(halves):
                            dve.wait_ge(s["exped"], 2 * b + half + 1)
                            own.add(nc.vector.tensor_reduce(rsum[:, 0, heads], exps, AX.X, ALU.add))
                        own.settle(dve)
                        own.add(nc.vector.reciprocal(rsum[:, 1, :], rsum[:, 0, :]))
                        own.settle(dve)
                        nc.vector.tensor_tensor(probs[:, pb, :, :], probs[:, pb, :, :],
                                                rsum[:, 1, :].unsqueeze(2).broadcast_to([P, HEADS, W2]),
                                                ALU.mult).then_inc(s["probs_ready"], 1)
                if live(SEQT * (g - 1)):
                    lp = layer_of(g - 1)
                    at_least(dve, s["f_made"], g - 1)
                    for c in range(FCH):
                        dve.wait_ge(s["gelu_made"], FCH * (g - 1) + c + 1)
                        nc.vector.scalar_tensor_tensor(hT[:, c, :], ring[0:FW, slot("H", c), 512:1024],
                                                       b1[:, lp, c:c + 1], gelu[:, c % 2, :], ALU.add,
                                                       ALU.mult).then_inc(s["h_ready"], 1)
                    own.settle(dve)

            rounds(dve, HEAD, TAIL, body, own, 8 * SEQT + 1)
            dve.wait_ge(s["x_done"], GROUPS)


def layer_norm_tiles(nc, src, dst, name):
    with ExitStack() as ctx:
        stats = ctx.enter_context(nc.sbuf_tensor(name + "_stats", [P, TILES, 6], F32))
        meanvar = ctx.enter_context(nc.sbuf_tensor(name + "_meanvar", [P, TILES, 2], F32))
        rstd = ctx.enter_context(nc.sbuf_tensor(name + "_rstd", [P, TILES], F32))
        power = ctx.enter_context(nc.sbuf_tensor(name + "_power", [P, TILES], F32))
        stats_made, var_made, var_eps, power_made, rstd_made, normed = (
            ctx.enter_context(nc.semaphore(f"{name}_{n}"))
            for n in ("stats_made", "var_made", "var_eps", "power_made", "rstd_made", "normed"))
        with nc.Block() as block:
            @block.vector
            def _(dve):
                for t in range(TILES):
                    nc.vector.bn_stats(stats[:, t, :], src[:, t, :]).then_inc(stats_made, 1)
                dve.wait_ge(stats_made, TILES)
                for t in range(TILES):
                    nc.vector.bn_aggr(meanvar[:, t, :], stats[:, t, :]).then_inc(var_made, 1)
                dve.wait_ge(var_made, TILES)
                nc.vector.tensor_scalar(rstd[:, :], meanvar[:, :, 1], EPS, None, ALU.add).then_inc(var_eps, 1)
                dve.wait_ge(rstd_made, 1)
                for t in range(TILES):
                    nc.vector.tensor_scalar(dst[:, t, :], src[:, t, :], meanvar[:, t, 0:1], rstd[:, t:t + 1],
                                            ALU.subtract, ALU.mult).then_inc(normed, 1)
                dve.wait_ge(normed, TILES)

            @block.gpsimd
            def _(pool):
                nc.gpsimd.memset(power[:, :], -0.5).then_inc(power_made, 1)
                pool.wait_ge(power_made, 1)
                pool.wait_ge(var_eps, 1)
                nc.gpsimd.tensor_tensor(rstd[:, :], rstd[:, :], power[:, :], ALU.pow).then_inc(rstd_made, 1)


def relative_attention(nc, x, w, scratch):
    with ExitStack() as ctx:
        def sb(name, shape, dt=F32):
            return ctx.enter_context(nc.sbuf_tensor(name, shape, dt))

        def sem(name):
            return ctx.enter_context(nc.semaphore("a_" + name))

        S = SEQ
        EDGE = P + 1
        HEADS_ALL = BATCH * H0
        STEPS = S // P
        consts = sb("consts", [P, 2, S])
        fcols = sb("fcols", [P, 2, S + 1])
        mask = sb("mask", [P, 2 * EDGE])
        ident = sb("ident_a", [P, P])
        wproj = sb("wproj", [P, 4, D])
        cols = sb("cols", [P, 8])
        rows = sb("rows", [P, 2, D])
        attn = sb("attn", [P, TILES, D])
        vaug = sb("vaug", [P, TILES, H0, DP + 1])

        with ExitStack() as first:
            def sb1(name, shape):
                return first.enter_context(nc.sbuf_tensor(name, shape, F32))

            def sem1(name):
                return first.enter_context(nc.semaphore("p_" + name))

            qvT, quT, kTs = sb1("qvT", [P, TILES * P + 1]), sb1("quT", [P, TILES * P]), sb1("kTs", [P, TILES * P])
            xnT = sb1("xnT_a", [P, TILES * P])
            bps = sb1("bps", [P, S])
            layer_norm_tiles(nc, x, attn, "norm1")
            ps = first.enter_context(nc.psum_tensor("ps_a", [P, 8, 512], F32))
            loaded, turned, copied, biases, q_made, k_made, v_made, q_read, k_read, v_read, filled, stored = (
                sem1(n) for n in ("loaded turned copied biases q_made k_made v_made q_read k_read v_read filled "
                                  "stored").split())
            with nc.Block() as block:
                @block.sync
                def _(sp):
                    for dst, src in ((consts[:, :, :], w["turns"]), (fcols[:, :, :], w["fcols"]), (mask[:, :], w["mask"]),
                                     (ident[:, :], w["ident"]), (wproj[:, :, :], w["wproj"]), (cols[:, :], w["cols"]),
                                     (rows[:, :, :], w["rows"])):
                        sp.dma_start(dst, src).then_inc(loaded, 16)
                    sp.wait_ge(q_read, 2 * BATCH)
                    sp.wait_ge(filled, 3)
                    sp.dma_start(scratch["qv"], qvT[:, :]).then_inc(stored, 16)
                    sp.dma_start(scratch["qu"], quT[:, :]).then_inc(stored, 16)
                    sp.dma_start(scratch["bp"], bps[:, :]).then_inc(stored, 16)
                    sp.wait_ge(k_read, BATCH)
                    sp.dma_start(scratch["k"], kTs[:, :]).then_inc(stored, 16)
                    sp.wait_ge(stored, 4 * 16)

                @block.tensor
                def _(pe):
                    pe.wait_ge(loaded, 7 * 16)
                    for t in range(TILES):
                        bank = t // 4
                        nc.tensor.transpose(ps[:, bank, (t % 4) * P:(t % 4 + 1) * P], attn[:, t, :],
                                            ident[:, :]).then_inc(turned, 1)
                    for b in range(BATCH):
                        pe.wait_ge(copied, b + 1)
                        nc.tensor.matmul(ps[:, 4 + b % 2, :], wproj[:, 0, :], xnT[:, b * S:(b + 1) * S],
                                         start=True, stop=True).then_inc(q_made, 1) if b < 2 else None
                        if b < 2:
                            nc.tensor.matmul(ps[:, 6 + b, :], wproj[:, 1, :], xnT[:, b * S:(b + 1) * S],
                                             start=True, stop=True).then_inc(k_made, 1)
                    for b in range(2, BATCH):
                        pe.wait_ge(q_read, 2 * (b - 1))
                        nc.tensor.matmul(ps[:, 4 + b % 2, :], wproj[:, 0, :], xnT[:, b * S:(b + 1) * S],
                                         start=True, stop=True).then_inc(q_made, 1)
                        pe.wait_ge(k_read, b - 1)
                        nc.tensor.matmul(ps[:, 6 + b % 2, :], wproj[:, 1, :], xnT[:, b * S:(b + 1) * S],
                                         start=True, stop=True).then_inc(k_made, 1)
                    for t in range(TILES):
                        nc.tensor.matmul(ps[:, t // 4, (t % 4) * D:(t % 4 + 1) * D], xnT[:, t * P:(t + 1) * P],
                                         wproj[:, 2, :], start=True, stop=True).then_inc(v_made, 1)

                @block.scalar
                def _(act):
                    for b in range(BATCH):
                        act.wait_ge(turned, 4 * (b + 1))
                        nc.scalar.copy(xnT[:, b * S:(b + 1) * S], ps[:, b, :]).then_inc(copied, 1)
                    act.wait_ge(biases, 2)
                    for b in range(BATCH):
                        act.wait_ge(q_made, b + 1)
                        for dst, bias in ((qvT, 7), (quT, 6)):
                            nc.scalar.activation(dst[:, b * S:(b + 1) * S], ps[:, 4 + b % 2, :], ACT.Identity,
                                                 bias=cols[:, bias:bias + 1]).then_inc(q_read, 1)

                @block.vector
                def _(dve):
                    dve.wait_ge(loaded, 7 * 16)
                    nc.vector.tensor_tensor(cols[:, 6:7], cols[:, 0:1], cols[:, 2:3], ALU.add).then_inc(biases, 1)
                    nc.vector.tensor_tensor(cols[:, 7:8], cols[:, 0:1], cols[:, 3:4], ALU.add).then_inc(biases, 1)
                    nc.vector.memset(qvT[:, TILES * P:TILES * P + 1], 0.0).then_inc(filled, 1)
                    nc.vector.memset(vaug[:, :, :, DP:DP + 1], 1.0).then_inc(filled, 1)
                    nc.vector.tensor_copy(bps[:, :], cols[:, 4:5].broadcast_to([P, S])).then_inc(filled, 1)
                    for b in range(BATCH):
                        dve.wait_ge(k_made, b + 1)
                        nc.vector.tensor_scalar(kTs[:, b * S:(b + 1) * S], ps[:, 6 + b % 2, :], cols[:, 1:2], None,
                                                ALU.add).then_inc(k_read, 1)
                    for b in range(BATCH):
                        dve.wait_ge(v_made, 4 * (b + 1))
                        for t in range(4 * b, 4 * b + 4):
                            nc.vector.tensor_tensor(
                                vaug[:, t, :, 0:DP],
                                ps[:, b, (t % 4) * D:(t % 4 + 1) * D].rearrange("p (h d) -> p h d", d=DP),
                                rows[:, 0, :].rearrange("p (h d) -> p h d", d=DP), ALU.add).then_inc(v_read, 1)
                    dve.wait_ge(v_read, TILES)

        with ExitStack() as second:
            def sb2(name, shape):
                return second.enter_context(nc.sbuf_tensor(name, shape, F32))

            below = sb2("below", [2 * DP, 2, S])
            above = sb2("above", [2 * DP, 2, S])
            keys = sb2("keys", [2 * DP, 2, S])
            keys0 = sb2("keys0", [2 * DP, 2, S])
            wpT = sb2("wpT", [DP, 2, 2, D])
            qpart = sb2("qpart", [P, 2, S])
            qrot = sb2("qrot", [P, 2, S + 1])
            edge2 = sb2("edge2", [P, 2, 2 * EDGE])
            edge = sb2("edge", [P, 2, EDGE])
            top = sb2("top", [P, 2])
            shift = sb2("shift", [P, 2])
            probs = sb2("probs_a", [P, 2, S])
            pT = sb2("pT_a", [P, 2, STEPS, S])
            vhead = sb2("vhead", [P, 2, STEPS, DP + 1])
            oT = sb2("oT_a", [P, S])
            inv = sb2("inv", [P, STEPS])
            ps = second.enter_context(nc.psum_tensor("ps_b", [P, 8, 512], F32))
            names = ("heads_in0 heads_in1 zeroed g_made g_turned qrot_made edge_made edge_masked edge_summed scored "
                     "topped exped p_turned p_copied vhead_made o_summed o_copied o_turned o_done stood dve_own").split()
            s = {n: sem(n) for n in names}
            LOADS = 8 * 16
            N = HEADS_ALL

            def live(n):
                return not isinstance(n, int) or 0 <= n < N

            def live_step(m):
                return not isinstance(m, int) or 0 <= m < STEPS * N

            with nc.Block() as block:
                @block.sync
                def _(sp):
                    def load(n, par):
                        b, h = n % BATCH, n // BATCH
                        of = bass.ds(h * DP, DP)
                        here, ahead = bass.ds(b * S, S), bass.ds(b * S + 1, S)
                        at_least(sp, s["scored"], STEPS * (n - 1))
                        stand(sp, s["stood"])
                        for dst, src in ((below[0:DP, par, :], scratch["qv"][of, here]),
                                         (below[DP:2 * DP, par, :], scratch["qu"][of, here]),
                                         (above[0:DP, par, :], scratch["qv"][of, ahead]),
                                         (above[DP:2 * DP, par, :], scratch["qu"][of, here]),
                                         (keys[0:DP, par, :], scratch["bp"][of, :]),
                                         (keys[DP:2 * DP, par, :], scratch["k"][of, here]),
                                         (keys0[DP:2 * DP, par, :], scratch["k"][of, here]),
                                         (wpT[:, par, :, :], w["wpT"][h])):
                            sp.dma_start(dst, src).then_inc(s[f"heads_in{par}"], 16)
                    sp.wait_ge(s["zeroed"], 3)
                    load(0, 0)
                    load(1, 1)
                    with sp.Fori(1, N // 2) as two:
                        load(2 * two, 0)
                        load(2 * two + 1, 1)

                def steps(body):
                    def round_(two):
                        for par in range(2):
                            n = 2 * two + par
                            for it in range(STEPS):
                                body(n, par, it, STEPS * n + it)
                    return round_

                def two_rounds(eng, body, own=None, each=0):
                    rounds(eng, (0,), (N // 2 - 1, N // 2), steps(body), own, each)

                @block.tensor
                def _(pe):
                    def turn(n, par):
                        pe.wait_ge(s[f"heads_in{par}"], LOADS * (n // 2 + 1))
                        at_least(pe, s["g_turned"], n)
                        at_least(pe, s["o_copied"], n - 1)
                        at_least(pe, s["o_done"], n - 2)
                        for half in range(2):
                            last = nc.tensor.matmul(ps[:, 4 + half, :], wpT[:, par, half, :], below[0:DP, par, :],
                                                    start=True, stop=True)
                        last.then_inc(s["g_made"], 1)

                    def edge_block(n, par, it, m):
                        if it == 0:
                            pe.wait_ge(s["qrot_made"], n + 1)
                        at_least(pe, s["edge_masked"], m - 1)
                        r = it * P
                        bank = ps[:, 2 + m_par(it), :]
                        for side, q, first in ((0, below, r), (1, above, r + 1)):
                            out = bank[:, side * EDGE:(side + 1) * EDGE]
                            nc.tensor.matmul(out, q[0:DP, par, r:r + P], keys[0:DP, par, 0:EDGE], start=True, stop=False)
                            last = nc.tensor.matmul(out, qrot[:, par, first:first + P], fcols[:, side, r:r + EDGE],
                                                    start=False, stop=True)
                        last.then_inc(s["edge_made"], 1)

                    def m_par(it):
                        return it % 2

                    def body(n, par, it, m):
                        if live(n):
                            at_least(pe, s["exped"], m - 1)
                            bank = ps[:, it % 2, :]
                            r = it * P
                            right = min(r + EDGE, S)
                            if r:
                                nc.tensor.matmul(bank[:, 0:r], below[:, par, r:r + P], keys[:, par, 0:r],
                                                 start=True, stop=False)
                                nc.tensor.matmul(bank[:, 0:r], qrot[:, par, r:r + P], fcols[:, 0, 0:r],
                                                 start=False, stop=True)
                            last = nc.tensor.matmul(bank[:, r:right], below[:, par, r:r + P], keys0[:, par, r:right],
                                                    start=True, stop=True)
                            if right < S:
                                nc.tensor.matmul(bank[:, right:S], above[:, par, r:r + P], keys[:, par, right:S],
                                                 start=True, stop=False)
                                last = nc.tensor.matmul(bank[:, right:S], qrot[:, par, r + 1:r + 1 + P],
                                                        fcols[:, 1, right:S], start=False, stop=True)
                            last.then_inc(s["scored"], 1)
                        if live_step(m - 1):
                            pe.wait_ge(s["exped"], m)
                            at_least(pe, s["p_copied"], m - 2)
                            for jt in range(STEPS):
                                last = nc.tensor.transpose(ps[:, 6 + (it + 1) % 2, jt * P:(jt + 1) * P],
                                                           probs[:, (it + 1) % 2, jt * P:(jt + 1) * P], ident[:, :])
                            last.then_inc(s["p_turned"], 1)
                        if it == 1 and live(n - 1):
                            pe.wait_ge(s["vhead_made"], n)
                            pe.wait_ge(s["p_copied"], STEPS * n)
                            pe.wait_ge(s["g_turned"], min(n + 1, N) if isinstance(n, int) else n + 1)
                            at_least(pe, s["o_copied"], n - 1)
                            for jt in range(STEPS):
                                last = nc.tensor.matmul(ps[0:DP + 1, 4, :], vhead[:, 1 - par, jt, :],
                                                        pT[:, 1 - par, jt, :], start=jt == 0, stop=jt == STEPS - 1)
                            last.then_inc(s["o_summed"], 1)
                        if it == 2 and live(n) and live(n + 1):
                            turn(n + 1, 1 - par)
                        if it == 3 and live(n - 1):
                            pe.wait_ge(s["o_copied"], n)
                            pe.wait_ge(s["g_turned"], min(n + 2, N) if isinstance(n, int) else n + 2)
                            at_least(pe, s["o_done"], n - 1)
                            for jt in range(STEPS):
                                last = nc.tensor.transpose(ps[:, 5, jt * P:(jt + 1) * P], oT[:, jt * P:(jt + 1) * P],
                                                           ident[:, :])
                            last.then_inc(s["o_turned"], 1)
                        nxt = (n, par, it + 1) if it + 1 < STEPS else (n + 1, 1 - par, 0)
                        if live(n) and live(nxt[0]):
                            edge_block(*nxt, m + 1)

                    pe.wait_ge(s["zeroed"], 3)
                    turn(0, 0)
                    edge_block(0, 0, 0, 0)
                    two_rounds(pe, body)

                @block.vector
                def _(dve):
                    own = Tally(s["dve_own"])

                    def turn(n, par):
                        dve.wait_ge(s["g_made"], n + 1)
                        at_least(dve, s["qrot_made"], n)
                        for half in range(2):
                            ins = nc.vector.tensor_tensor(qpart[:, half, :], ps[:, 4 + half, :], consts[:, half, :], ALU.mult)
                        ins.then_inc(s["g_turned"], 1)

                    def mask_edge(it, m):
                        dve.wait_ge(s["edge_made"], m + 1)
                        at_least(dve, s["edge_summed"], m - 1)
                        nc.vector.tensor_tensor(edge2[:, it % 2, :], ps[:, 2 + it % 2, 0:2 * EDGE], mask[:, :],
                                                ALU.mult).then_inc(s["edge_masked"], 1)

                    def body(n, par, it, m):
                        if live(n):
                            r = it * P
                            right = min(r + EDGE, S)
                            bank = ps[:, it % 2, :]
                            dve.wait_ge(s["scored"], m + 1)
                            dve.wait_ge(s["edge_summed"], m + 1)
                            own.add(nc.vector.tensor_tensor(bank[:, r:right], bank[:, r:right], edge[:, it % 2, 0:right - r],
                                                            ALU.add))
                            own.settle(dve)
                            own.add(nc.vector.tensor_reduce(top[:, it % 2:it % 2 + 1], bank, AX.X, ALU.max))
                            own.settle(dve)
                            at_least(dve, s["exped"], m - 1)
                            nc.vector.tensor_scalar(shift[:, it % 2:it % 2 + 1], top[:, it % 2:it % 2 + 1], -SCALE0, None,
                                                    ALU.mult).then_inc(s["topped"], 1)
                        if it == 2 and live(n) and live(n + 1):
                            turn(n + 1, 1 - par)
                        if live(n) and (it + 1 < STEPS or live(n + 1)):
                            mask_edge(it + 1, m + 1)
                        if it == 3 and live(n - 1):
                            b, h = (n - 1) % BATCH, (n - 1) // BATCH
                            dve.wait_ge(s["o_turned"], n)
                            o = ps[:, 5, :].rearrange("p (t d) -> p t d", d=P)
                            own.add(nc.vector.reciprocal(inv[:, :], o[:, :, DP]))
                            own.settle(dve)
                            nc.vector.tensor_tensor(attn[:, bass.ds(b * STEPS, STEPS), bass.ds(h * DP, DP)],
                                                    o[:, :, 0:DP], inv[:, :].unsqueeze(2).broadcast_to([P, STEPS, DP]),
                                                    ALU.mult).then_inc(s["o_done"], 1)

                    nc.vector.memset(keys0[0:DP, :, :], 0.0).then_inc(s["zeroed"], 1)
                    nc.vector.memset(qrot[:, :, S:S + 1], 0.0).then_inc(s["zeroed"], 1)
                    nc.vector.memset(oT[:, :], 0.0).then_inc(s["zeroed"], 1)
                    turn(0, 0)
                    mask_edge(0, 0)
                    two_rounds(dve, body, own, 2 * (2 * STEPS + 1))
                    dve.wait_ge(s["o_done"], N)

                @block.gpsimd
                def _(pool):
                    def turn(n, par):
                        pool.wait_ge(s["g_turned"], n + 1)
                        at_least(pool, s["scored"], STEPS * (n - 1))
                        nc.gpsimd.tensor_tensor(qrot[:, par, 0:S], qpart[:, 0, :], qpart[:, 1, :],
                                                ALU.add).then_inc(s["qrot_made"], 1)

                    def sum_edge(it, m):
                        pool.wait_ge(s["edge_masked"], m + 1)
                        at_least(pool, s["topped"], m - 1)
                        nc.gpsimd.tensor_tensor(edge[:, it % 2, :], edge2[:, it % 2, 0:EDGE], edge2[:, it % 2, EDGE:2 * EDGE],
                                                ALU.add).then_inc(s["edge_summed"], 1)

                    def body(n, par, it, m):
                        if it == 2 and live(n) and live(n + 1):
                            turn(n + 1, 1 - par)
                        if live(n) and (it + 1 < STEPS or live(n + 1)):
                            sum_edge(it + 1, m + 1)
                        if it == 0 and live(n):
                            b, h = n % BATCH, n // BATCH
                            at_least(pool, s["o_summed"], n - 1)
                            nc.gpsimd.tensor_copy(vhead[:, par, :, :], vaug[:, bass.ds(b * STEPS, STEPS), h, :]
                                                  ).then_inc(s["vhead_made"], 1)

                    turn(0, 0)
                    sum_edge(0, 0)
                    two_rounds(pool, body)

                @block.scalar
                def _(act):
                    def body(n, par, it, m):
                        if live(n):
                            act.wait_ge(s["topped"], m + 1)
                            at_least(act, s["p_turned"], m - 1)
                            nc.scalar.activation(probs[:, it % 2, :], ps[:, it % 2, :], ACT.Exp, scale=SCALE0,
                                                 bias=shift[:, it % 2:it % 2 + 1]).then_inc(s["exped"], 1)
                        if (live(n) and it) or live(n - 1) and it == 0:
                            hp, bt = (par, it - 1) if it else (1 - par, STEPS - 1)
                            act.wait_ge(s["p_turned"], m)
                            if it == 1:
                                at_least(act, s["o_summed"], n - 1)
                            nc.scalar.copy(pT[:, hp, :, bt * P:(bt + 1) * P],
                                           ps[:, 6 + bt % 2, :].rearrange("p (j c) -> p j c", c=P)
                                           ).then_inc(s["p_copied"], 1)
                        if it == 1 and live(n - 1):
                            act.wait_ge(s["o_summed"], n)
                            act.wait_ge(s["zeroed"], 3)
                            at_least(act, s["o_turned"], n - 1)
                            nc.scalar.copy(oT[0:DP + 1, :], ps[0:DP + 1, 4, :]).then_inc(s["o_copied"], 1)
                    two_rounds(act, body)

        with ExitStack() as third:
            aT = third.enter_context(nc.sbuf_tensor("aT", [P, TILES, P], F32))
            ps = third.enter_context(nc.psum_tensor("ps_c", [P, 8, 512], F32))
            turned, copied, projected, added = (sem("c_" + n) for n in ("turned", "copied", "projected", "added"))
            with nc.Block() as block:
                @block.tensor
                def _(pe):
                    for t in range(TILES):
                        nc.tensor.transpose(ps[:, t // 4, (t % 4) * P:(t % 4 + 1) * P], attn[:, t, :],
                                            ident[:, :]).then_inc(turned, 1)
                    for t in range(TILES):
                        pe.wait_ge(copied, t // 4 + 1)
                        nc.tensor.matmul(ps[:, 4 + t // 4, (t % 4) * D:(t % 4 + 1) * D], aT[:, t, :], wproj[:, 3, :],
                                         start=True, stop=True).then_inc(projected, 1)

                @block.scalar
                def _(act):
                    for b in range(BATCH):
                        act.wait_ge(turned, 4 * (b + 1))
                        nc.scalar.copy(aT[:, 4 * b:4 * b + 4, :].rearrange("p t c -> p (t c)"),
                                       ps[:, b, :]).then_inc(copied, 1)

                @block.vector
                def _(dve):
                    tiles = x[:, :, :]
                    nc.vector.tensor_tensor(tiles, tiles, rows[:, 1:2, :].broadcast_to([P, TILES, D]),
                                            ALU.add).then_inc(added, 1)
                    dve.wait_ge(added, 1)
                    for b in range(BATCH):
                        dve.wait_ge(projected, 4 * (b + 1))
                        tiles = x[:, 4 * b:4 * b + 4, :].rearrange("p t d -> p (t d)")
                        nc.vector.tensor_tensor(tiles, ps[:, 4 + b, :], tiles, ALU.add).then_inc(added, 1)
                    dve.wait_ge(added, 1 + BATCH)


def whole_kernel(nc, x_in, out, attention, layers):
    with ExitStack() as ctx:
        x1 = ctx.enter_context(nc.sbuf_tensor("x1", [P, TILES, D], F32))
        x = ctx.enter_context(nc.sbuf_tensor("x", [P, TILES, D], F32))
        x_loaded, added, stored = (ctx.enter_context(nc.semaphore(n)) for n in ("x_loaded", "x_added", "out_stored"))
        scratch = {n: nc.dram_tensor("scratch_" + n, [P, c], F32).ap()
                   for n, c in (("qv", TILES * P + 1), ("qu", TILES * P), ("k", TILES * P), ("bp", SEQ))}
        tiled = "(t p) d -> p t d"
        with nc.Block() as block:
            @block.sync
            def _(sp):
                sp.dma_start(x1[:, :, :], x_in.rearrange("b s d -> (b s) d").rearrange(tiled, p=P)).then_inc(x_loaded, 16)
                sp.wait_ge(x_loaded, 16)
        relative_attention(nc, x1, attention, scratch)
        layer_norm_tiles(nc, x1, x, "norm2")
        local_layers(nc, x, layers)
        with nc.Block() as block:
            @block.vector
            def _(dve):
                nc.vector.tensor_tensor(x[:, :, :], x[:, :, :], x1[:, :, :], ALU.add).then_inc(added, 1)

            @block.sync
            def _(sp):
                sp.wait_ge(added, 1)
                sp.dma_start(out.rearrange("b s d -> (b s) d").rearrange(tiled, p=P), x[:, :, :]).then_inc(stored, 16)
                sp.wait_ge(stored, 16)


def attention_layout(a):
    import numpy as np

    freq = 1.0 / 10000.0 ** (2.0 * np.arange(D // 2, dtype=np.float64) / D)
    turn = -(1.0 + np.arange(SEQ, dtype=np.float64))[None, :] * freq[:, None]
    col = np.arange(SEQ + 1, dtype=np.float64)[None, :]
    fcols = [np.concatenate([np.sin((col + off) * freq[:, None]), np.cos((col + off) * freq[:, None])]) for off in (SEQ, 0)]
    i, j = np.arange(P)[:, None], np.arange(P + 1)[None, :]
    wp = a["Wp"].reshape(D, H0, DP).transpose(1, 2, 0)
    cols = np.zeros((P, 8), np.float32)
    for n, c in enumerate((a["bq"], a["bk"], a["u"].reshape(-1), a["v"].reshape(-1), a["bp"])):
        cols[:, n] = c
    return {
        "turns": np.stack([np.concatenate([np.cos(turn)] * 2), np.concatenate([-np.sin(turn), np.sin(turn)])], 1
                          ).astype(np.float32),
        "fcols": np.stack(fcols, 1).astype(np.float32),
        "mask": np.concatenate([j <= i, j >= i + 2], 1).astype(np.float32),
        "ident": np.eye(P, dtype=np.float32),
        "wproj": np.stack([a[n] for n in ("Wq", "Wk", "Wv", "Wo")], 1),
        "cols": cols,
        "rows": np.broadcast_to(np.stack([a["bv"], a["bo"]])[None], (P, 2, D)),
        "wpT": np.stack([wp, np.concatenate([wp[:, :, D // 2:], wp[:, :, :D // 2]], 2)], 2),
    }


def layers_layout(f):
    import numpy as np

    w1 = np.zeros((DEPTH, D, 2, FCH * FW), np.float32)
    w1[:, :, :, :DFF] = f["W1"].reshape(DEPTH, D, 2, DFF)
    b1 = np.zeros((DEPTH, 2, FCH * FW), np.float32)
    b1[:, :, :DFF] = f["b1"].reshape(DEPTH, 2, DFF)
    w2 = np.zeros((DEPTH, FCH * FW, D), np.float32)
    w2[:, :DFF] = f["W2"]
    half = np.arange(0, DH, 2, dtype=np.float64)
    t = np.arange(SEQ, dtype=np.float64)
    freqs = np.concatenate([t[:, None] * (1.0 / 10000.0 ** (half / DH))[None, :]] * 2, -1)
    base = (half + 0.4 * DH) / (1.4 * DH)
    scale = np.concatenate([base[None, :] ** ((t - SEQ // 2) / (W // 2))[:, None]] * 2, -1)
    sign = np.where(np.arange(DH) < DH // 2, 1.0, -1.0)
    rope = np.empty((P, 2, SEQT * 2, DH), np.float32)
    for n, sc in enumerate((scale, 1.0 / scale)):
        for part, table in enumerate((np.cos(freqs) * sc, np.sin(freqs) * sc * sign)):
            rope[:, n, part::2, :] = table.reshape(SEQT, P, DH).transpose(1, 0, 2)
    return {
        "wqkv": f["Wqkv"],
        "wo": f["Wo"].reshape(DEPTH, PAIRS // 2, 2, 2, DH, D).transpose(0, 2, 4, 1, 3, 5).reshape(DEPTH, P, PAIRS, D),
        "w1": w1.reshape(DEPTH, D, 2 * FCH * FW),
        "w2": w2.reshape(DEPTH, FCH, FW, D).transpose(0, 2, 1, 3),
        "b1": b1.reshape(DEPTH, 2 * FCH, FW).transpose(0, 2, 1),
        "ln": np.stack([f["ln_g"], f["ln_b"]], -1),
        "b2": np.broadcast_to(f["b2"][:, None, :], (DEPTH, P, D)),
        "qk": np.broadcast_to(np.stack([f["q_scale"], f["k_scale"]], 1)[:, None], (DEPTH, P, 2, DH)),
        "rope": rope,
        "ident": np.eye(P, dtype=np.float32),
    }


def kernel(**inputs):
    import numpy as np
    import concourse.bacc as bacc
    from concourse.bass_utils import run_bass_kernel_spmd

    parts = {}
    for group, prefix, layout in (("a", "L0_attn_", attention_layout), ("l", "L0_ffn_", layers_layout)):
        parts[group] = layout({n[len(prefix):]: np.asarray(a) for n, a in inputs.items()
                               if n.startswith(prefix) and n != "L0_attn_x"})
    nc = bacc.Bacc("TRN2", target_bir_lowering=False, num_devices=1)
    arrays, aps = {}, {}

    def declare(name, a):
        arrays[name] = np.ascontiguousarray(a)
        return nc.dram_tensor(name, arrays[name].shape, mybir.dt.from_np(arrays[name].dtype), kind="ExternalInput").ap()

    x_in = declare("in_x", np.asarray(inputs["L0_attn_x"]))
    for group, named in parts.items():
        aps[group] = {n: declare(f"in_{group}_{n}", a) for n, a in named.items()}
    out = nc.dram_tensor("out_0_dram", (BATCH, SEQ, D), F32, kind="ExternalOutput").ap()
    whole_kernel(nc, x_in, out, aps["a"], aps["l"])
    r = run_bass_kernel_spmd(nc, [arrays], core_ids=[0])
    return r.results[0]["out_0_dram"]
```
